# Optimizing a Trainium2 kernel written in Bass

```python
import numpy as np
import jax
import jax.numpy as jnp

def _softmax(x, axis=-1):
    return jax.nn.softmax(x, axis=axis)

def _gelu(x):
    return jax.nn.gelu(x, approximate=True)

def _silu(x):
    return jax.nn.silu(x)

def _sigmoid(x):
    return jax.nn.sigmoid(x)

def _layernorm(x, axis=-1, eps=1e-05):
    m = jnp.mean(x, axis=axis, keepdims=True)
    v = jnp.var(x, axis=axis, keepdims=True)
    return (x - m) / jnp.sqrt(v + eps)

def _scatter_add(tgt, idx, src, axis=0):
    return tgt.at[idx].add(src)

def _segment_sum(src, seg, n):
    return jax.ops.segment_sum(src, seg, n)
kernel_name = 'mk_seq_postln_d1_jaxref_r4_168f1f'

def setup_inputs(seed: int=0):
    np.random.seed(seed)
    _w = jnp.asarray

    def _L0_attn_setup():
        import jax, jax.numpy as jnp
        import numpy as np
        EMBED_DIM = 256
        NUM_HEADS = 16
        HEAD_DIM = EMBED_DIM // NUM_HEADS

        def _kernel_exp(x):
            return jnp.exp(x - jnp.max(x, axis=-1, keepdims=True))
        key = jax.random.key(seed)
        ks = jax.random.split(key, 9)
        s = 1.0 / np.sqrt(EMBED_DIM)
        inp = {'x': jax.random.normal(ks[0], (4, 2048, EMBED_DIM), dtype=jnp.float32)}
        for i, name in enumerate(['q', 'k', 'v', 'o']):
            inp[f'W{name}'] = jax.random.uniform(ks[1 + 2 * i], (EMBED_DIM, EMBED_DIM), jnp.float32, -s, s)
            inp[f'b{name}'] = jax.random.uniform(ks[2 + 2 * i], (EMBED_DIM,), jnp.float32, -s, s)
        return inp
    _L0_attn_in = _L0_attn_setup()

    def _L0_ffn_setup():
        import jax, jax.numpy as jnp
        import numpy as np
        EPS = 1e-05

        def _quantize(W):
            gamma = jnp.mean(jnp.abs(W))
            return jnp.clip(jnp.round(W / (gamma + EPS)), -1.0, 1.0)
        key = jax.random.key(seed)
        k_x, k_w1, k_b1, k_w2, k_b2 = jax.random.split(key, 5)
        n_embd = 256
        d_ff = 4 * n_embd
        B, S = (4, 1024)
        bound1 = 1.0 / np.sqrt(n_embd)
        bound2 = 1.0 / np.sqrt(d_ff)
        x = jax.random.normal(k_x, (B, S, n_embd), dtype=jnp.float32)
        W1 = jax.random.uniform(k_w1, (d_ff, n_embd), jnp.float32, -bound1, bound1)
        b1 = jax.random.uniform(k_b1, (d_ff,), jnp.float32, -bound1, bound1)
        W2 = jax.random.uniform(k_w2, (n_embd, d_ff), jnp.float32, -bound2, bound2)
        b2 = jax.random.uniform(k_b2, (n_embd,), jnp.float32, -bound2, bound2)
        return {'x': x, 'W1': W1, 'b1': b1, 'W2': W2, 'b2': b2}
    _L0_ffn_in = _L0_ffn_setup()
    _d = {'L0_attn_x': _L0_attn_in['x'], 'L0_attn_Wq': _L0_attn_in['Wq'], 'L0_attn_bq': _L0_attn_in['bq'], 'L0_attn_Wk': _L0_attn_in['Wk'], 'L0_attn_bk': _L0_attn_in['bk'], 'L0_attn_Wv': _L0_attn_in['Wv'], 'L0_attn_bv': _L0_attn_in['bv'], 'L0_attn_Wo': _L0_attn_in['Wo'], 'L0_attn_bo': _L0_attn_in['bo'], 'L0_ffn_W1': _L0_ffn_in['W1'], 'L0_ffn_b1': _L0_ffn_in['b1'], 'L0_ffn_W2': _L0_ffn_in['W2'], 'L0_ffn_b2': _L0_ffn_in['b2']}
    _x0 = _d['L0_attn_x']
    _d['L0_attn_x'] = jax.random.normal(jax.random.fold_in(jax.random.key(seed), 1), (16, 512, 256), dtype=_x0.dtype)
    del _x0
    return _d

def reference(L0_attn_x, L0_attn_Wq, L0_attn_bq, L0_attn_Wk, L0_attn_bk, L0_attn_Wv, L0_attn_bv, L0_attn_Wo, L0_attn_bo, L0_ffn_W1, L0_ffn_b1, L0_ffn_W2, L0_ffn_b2):

    def _L0_attn_ref(x, Wq, bq, Wk, bk, Wv, bv, Wo, bo):
        import jax, jax.numpy as jnp
        import numpy as np
        EMBED_DIM = 256
        NUM_HEADS = 16
        HEAD_DIM = EMBED_DIM // NUM_HEADS

        def _kernel_exp(x):
            return jnp.exp(x - jnp.max(x, axis=-1, keepdims=True))
        b, s, e = x.shape

        def proj(W, bias):
            return (x @ W.T + bias).reshape(b, s, NUM_HEADS, HEAD_DIM).transpose(0, 2, 1, 3)
        q = proj(Wq, bq)
        k = proj(Wk, bk)
        v = proj(Wv, bv)
        q_kern = _kernel_exp(q)
        k_kern = _kernel_exp(k)
        kv = jnp.einsum('bhsd,bhse->bhde', k_kern, v)
        k_sum = jnp.sum(k_kern, axis=2)
        denom = jnp.einsum('bhqd,bhd->bhq', q_kern, k_sum) + 1e-06
        y = jnp.einsum('bhqd,bhde->bhqe', q_kern, kv) / denom[..., None]
        y = y.transpose(0, 2, 1, 3).reshape(b, s, e)
        return y @ Wo.T + bo

    def _L0_ffn_ref(x, W1, b1, W2, b2):
        import jax, jax.numpy as jnp
        import numpy as np
        EPS = 1e-05

        def _quantize(W):
            gamma = jnp.mean(jnp.abs(W))
            return jnp.clip(jnp.round(W / (gamma + EPS)), -1.0, 1.0)
        Wq1 = _quantize(W1)
        Wq2 = _quantize(W2)
        h = jax.nn.relu(jnp.einsum('bsd,fd->bsf', x, Wq1) + b1)
        out = jnp.einsum('bsf,df->bsd', h, Wq2) + b2
        return out
    x = L0_attn_x
    x = _layernorm(x + _L0_attn_ref(x, L0_attn_Wq, L0_attn_bq, L0_attn_Wk, L0_attn_bk, L0_attn_Wv, L0_attn_bv, L0_attn_Wo, L0_attn_bo), axis=-1)
    x = _layernorm(x + _L0_ffn_ref(x, L0_ffn_W1, L0_ffn_b1, L0_ffn_W2, L0_ffn_b2), axis=-1)
    return x

_drawn_inputs = setup_inputs


def setup_inputs(seed=0):
    import zlib

    import numpy as np

    out = dict(_drawn_inputs(seed))
    spreads = {}
    factors = {'L0_attn_Wq': 8.0,
     'L0_attn_bq': 24.817,
     'L0_attn_Wk': 8.0,
     'L0_attn_bk': 23.091,
     'L0_attn_Wv': 3.863,
     'L0_attn_bv': 2.863,
     'L0_ffn_b1': 21.866,
     'L0_ffn_b2': 64.0}
    for name, (base, spread) in spreads.items():
        noise = np.random.default_rng([zlib.crc32(name.encode()), seed]).standard_normal(out[name].shape)
        drawn = base * np.exp(spread * noise) if base else spread * noise
        out[name] = jnp.asarray(drawn.astype(out[name].dtype))
    for name, factor in factors.items():
        out[name] = (out[name] * factor).astype(out[name].dtype)
    return out
```

```python
from contextlib import ExitStack

import numpy as np

import concourse.bass as bass
from concourse import mybir

F32 = mybir.dt.float32
F32R = mybir.dt.float32r
ALU = mybir.AluOpType
ACT = mybir.ActivationFunctionType
AX_X = mybir.AxisListType.X

P = 128
LN_EPS = 1e-5
Q_EPS = 1e-5
DEN_EPS = 1e-6


def attention_ffn_block(nc, x, x_t, wqk_t, bqk, wv_t, bv, wo_t, bo, w1_t, b1, w2_t, b2, ident_c, mask_c, out):
    NB, S, D = x.shape
    F = w1_t.shape[1]
    HEADS = 16
    HD = D // HEADS
    NJ = S // P
    ND = D // P
    NF = F // P
    HPC = P // HD
    HX = HD + 1
    NR = 4
    assert NJ == 4 and ND == 2 and NB % 2 == 0 and NB >= 4

    with ExitStack() as ctx:
        def sb(name, shape, dt=F32):
            return ctx.enter_context(nc.sbuf_tensor(name, shape, dt))

        def sem(name):
            return ctx.enter_context(nc.semaphore(name))

        wqk = sb("wqk", [P, ND, 2 * D])
        wv = sb("wv", [P, ND, D])
        wo = sb("wo", [P, ND, D])
        w1 = sb("w1", [P, ND * F])
        w2 = sb("w2", [P, NF * D])
        w1q = sb("w1q", [P, ND * F], F32R)
        w2q = sb("w2q", [P, NF * D], F32R)
        below = sb("below", [P, ND * F])
        bqk_rows = sb("bqk_rows", [P, 2 * D])
        bo_rows = sb("bo_rows", [P, D])
        b2_rows = sb("b2_rows", [P, D])
        bv_rows = sb("bv_rows", [P, D])
        b1_col = sb("b1_col", [P, NF])
        ident = sb("ident", [P, P])
        mask = sb("mask", [P, HEADS])
        bv_mask = sb("bv_mask", [P, HEADS, HX])
        ones = sb("ones", [P, P])
        minus_half = sb("minus_half", [P, NJ])
        wsum = sb("wsum", [P, 2])
        thr = sb("thr", [P, 2])
        neg_thr = sb("neg_thr", [P, 2])

        xs = [sb(f"xs{p}", [P, NJ, D]) for p in range(2)]
        xt = [sb(f"xt{p}", [P, ND, S]) for p in range(2)]
        x_bo = sb("x_bo", [P, NJ, D])
        qk_pre = sb("qk_pre", [P, 2, 2 * D])
        qk_max = sb("qk_max", [P, 2, 2 * HEADS])
        qk_exp = sb("qk_exp", [P, NJ, 2 * D])
        k_pair = sb("k_pair", [P, 2, D])
        k_tok = sb("k_tok", [P, D])
        gt = sb("gt", [P, ND, D])
        kv_cut = sb("kv_cut", [P, HEADS, HX])
        k_sum = sb("k_sum", [P, ND])
        kv = sb("kv", [P, HEADS, HX])
        q_t = sb("q_t", [P, ND, S])
        den = sb("den", [P, NJ, HEADS])
        rden = sb("rden", [P, NJ, HEADS])
        y = sb("y", [P, NJ, D])
        y_t = sb("y_t", [P, ND, S])
        r1 = sb("r1", [P, NJ, D])
        st1 = sb("st1", [P, NJ, 6])
        mv1 = sb("mv1", [P, NJ, 2])
        ve1 = sb("ve1", [P, NJ])
        rstd1 = sb("rstd1", [P, NJ])
        x1 = sb("x1", [P, NJ, D])
        x1_b2 = sb("x1_b2", [P, NJ, D])
        x1_hi = sb("x1_hi", [P, ND, S], F32R)
        x1_lo = sb("x1_lo", [P, ND, S], F32R)
        h_full = sb("h_full", [P, NR, S])
        h_hi = sb("h_hi", [P, NF, S], F32R)
        h_lo = sb("h_lo", [P, NF, S], F32R)
        r2 = sb("r2", [P, NJ, D])
        st2 = sb("st2", [P, NJ, 6])
        mv2 = sb("mv2", [P, NJ, 2])
        ve2 = sb("ve2", [P, NJ])
        rstd2 = sb("rstd2", [P, NJ])
        res = [sb(f"res{p}", [P, NJ, D]) for p in range(2)]

        ps = ctx.enter_context(nc.psum_tensor("ps", [P, 8, 512], F32))
        WORK = 0
        MID = 2
        TOK = 4
        TRN = 6
        F1_BANKS = (WORK, WORK + 1, TRN, TRN + 1)
        YW = HEADS * HX
        KS = D

        s_w = {n: sem(f"s_{n}") for n in ("wqk", "bqk", "wv", "ident", "mask", "bv", "bo", "wo", "w1", "w2", "b1", "b2")}
        s_x = [sem(f"s_x{p}") for p in range(2)]
        s_xt = [sem(f"s_xt{p}") for p in range(2)]
        s_out = [sem(f"s_out{p}") for p in range(2)]
        const_set = sem("const_set")
        w_abs = sem("w_abs")
        w_total = sem("w_total")
        w_thr = sem("w_thr")
        w_below = sem("w_below")
        w_quant = sem("w_quant")
        bvm_ready = sem("bvm_ready")
        qk_done = sem("qk_done")
        qk_added = sem("qk_added")
        qk_maxed = sem("qk_maxed")
        qk_shift = sem("qk_shift")
        exp_done = sem("exp_done")
        g_done = sem("g_done")
        gt_ready = sem("gt_ready")
        qt_done = sem("qt_done")
        qt_ready = sem("qt_ready")
        k_paired = sem("k_paired")
        k_tok_ready = sem("k_tok_ready")
        kv_done = sem("kv_done")
        kv_cut_done = sem("kv_cut_done")
        kv_ready = sem("kv_ready")
        y_done = sem("y_done")
        den_out = sem("den_out")
        den_inv = sem("den_inv")
        y_ready = sem("y_ready")
        yt_done = sem("yt_done")
        yt_ready = sem("yt_ready")
        o_done = sem("o_done")
        xbo_ready = sem("xbo_ready")
        r1_done = sem("r1_done")
        st1_done = sem("st1_done")
        mv1_done = sem("mv1_done")
        ve1_done = sem("ve1_done")
        rstd1_done = sem("rstd1_done")
        x1_ready = sem("x1_ready")
        x1b2_ready = sem("x1b2_ready")
        x1t_done = sem("x1t_done")
        x1hi_ready = sem("x1hi_ready")
        x1lo_ready = sem("x1lo_ready")
        f1_done = sem("f1_done")
        h_ready = sem("h_ready")
        hhi_odd = sem("hhi_odd")
        hlo_ready = sem("hlo_ready")
        f2_done = sem("f2_done")
        r2_done = sem("r2_done")
        st2_done = sem("st2_done")
        mv2_done = sem("mv2_done")
        ve2_done = sem("ve2_done")
        rstd2_done = sem("rstd2_done")
        res_ready = sem("res_ready")

        def run_slots(eng, slot, peeled=1, last_looped=NB - 2):
            for b in range(peeled):
                slot(b // 2, b % 2)
            with eng.Fori(peeled // 2, last_looped // 2) as k:
                slot(k, 1)
                slot(k + 1, 0)
            for b in range(last_looped + 1, NB):
                slot(b // 2, b % 2)

        block = ctx.enter_context(nc.Block())

        @block.sync
        def _(sp):
            def load(b, k, p):
                sp.dma_start(xt[p][:, :, :], x_t[b].rearrange("(c p) t -> p c t", p=P)).then_inc(s_xt[p], 16)
                sp.dma_start(xs[p][:, :, :], x[b].rearrange("(p j) c -> p j c", j=NJ)).then_inc(s_x[p], 16)

            def weight(name, dst, src):
                sp.dma_start(dst, src).then_inc(s_w[name], 16)

            weight("wqk", wqk[:, :, :], wqk_t.rearrange("(c p) n -> p c n", p=P))
            load(0, 0, 0)
            weight("bqk", bqk_rows[:, :], bqk.to_broadcast([P, 2 * D]))
            weight("w1", w1[:, :].rearrange("p (c n) -> p c n", c=ND), w1_t.rearrange("(c p) n -> p c n", p=P))
            weight("w2", w2[:, :].rearrange("p (c n) -> p c n", c=NF), w2_t.rearrange("(c p) n -> p c n", p=P))
            weight("ident", ident[:, :], ident_c)
            weight("mask", mask[:, :], mask_c)
            weight("bv", bv_rows[:, :], bv.to_broadcast([P, D]))
            weight("wv", wv[:, :, :], wv_t.rearrange("(c p) n -> p c n", p=P))
            weight("bo", bo_rows[:, :], bo.to_broadcast([P, D]))
            weight("wo", wo[:, :, :], wo_t.rearrange("(c p) n -> p c n", p=P))
            weight("b1", b1_col[:, :], b1)
            weight("b2", b2_rows[:, :], b2.to_broadcast([P, D]))
            load(1, 0, 1)

            def store(m, k, p):
                sp.wait_ge(res_ready, NJ * m + NJ)
                sp.dma_start(out[m].rearrange("(p j) c -> p j c", j=NJ), res[p][:, :, :]).then_inc(s_out[p], 16)

            def slot(k, p):
                b = 2 * k + p
                looped = not isinstance(b, int)
                if looped or b + 2 < NB:
                    sp.wait_ge(g_done, b + 1)
                    sp.wait_ge(xbo_ready, b + 1)
                    sp.wait_ge(qk_done, NJ * b + NJ)
                    load(b + 2, k + 1, p)
                if looped or b > 0:
                    store(b - 1, k - 1 + p, 1 - p)

            run_slots(sp, slot, last_looped=NB - 4)
            store(NB - 1, NB // 2 - 1, 1)
            for p in range(2):
                sp.wait_ge(s_out[p], 16 * (NB // 2))

        @block.tensor
        def _(pe):
            def mm(dst, lhs, rhs, start, stop):
                return nc.tensor.matmul(dst, lhs, rhs, start=start, stop=stop)

            def qk_tile(n, kn, pn, j):
                bank = ps[:, WORK + j % 2, :]
                if j >= 2:
                    pe.wait_ge(qk_added, NJ * n + j - 1)
                for c in range(ND):
                    last = mm(bank, xt[pn][:, c, j * P:(j + 1) * P], wqk[:, c, :], c == 0, c == ND - 1)
                last.then_inc(qk_done, 1)

            def g_and_qt(n, kn, pn, first):
                pe.wait_ge(exp_done, NJ * n + NJ)
                pe.wait_ge(s_x[pn], 16 * (kn + 1))
                if not first:
                    pe.wait_ge(r1_done, 2 * n - 1)
                for c in range(ND):
                    for j in range(NJ):
                        last = mm(ps[:, MID, c * D:(c + 1) * D], xs[pn][:, j, c * P:(c + 1) * P],
                                  qk_exp[:, j, D:2 * D], j == 0, j == NJ - 1)
                last.then_inc(g_done, 1)
                if first:
                    pe.wait_ge(s_w["ident"], 16)
                elif not isinstance(n, int) or n > 1:
                    pe.wait_ge(r2_done, 2 * n - 2)
                for c in range(ND):
                    for j in range(NJ):
                        last = nc.tensor.transpose(ps[:, TOK + c, j * P:(j + 1) * P],
                                                   qk_exp[:, j, c * P:(c + 1) * P], ident[:, :])
                    last.then_inc(qt_done, 1)

            def k_sum_and_kv(n, first):
                if first:
                    pe.wait_ge(const_set, 3)
                    pe.wait_ge(s_w["wv"], 16)
                pe.wait_ge(k_tok_ready, n + 1)
                if not first:
                    pe.wait_ge(r1_done, 2 * n)
                for c in range(ND):
                    mm(ps[:, MID + 1, KS + c:KS + c + 1], k_tok[:, c * P:(c + 1) * P], ones[:, 0:1], True, True)
                pe.wait_ge(gt_ready, n + 1)
                for h in range(ND):
                    for c in range(ND):
                        last = mm(ps[:, MID + 1, h * P:(h + 1) * P], gt[:, c, h * P:(h + 1) * P],
                                  wv[:, c, h * P:(h + 1) * P], c == 0, c == ND - 1)
                last.then_inc(kv_done, 1)

            def ffn1(b, chunks):
                for f in chunks:
                    if f >= NR:
                        pe.wait_ge(h_ready, NF * b + f - NR + 1)
                    for c in range(ND):
                        for part in (x1_hi, x1_lo):
                            last = mm(ps[:, F1_BANKS[f % NR], :], w1q[:, c * F + f * P:c * F + (f + 1) * P],
                                      part[:, c, :], c == 0 and part is x1_hi, c == ND - 1 and part is x1_lo)
                    last.then_inc(f1_done, 1)

            def ffn2(m):
                pe.wait_ge(hlo_ready, NF * m + NF)
                for j in range(NJ):
                    for f in range(NF):
                        for part in (h_hi, h_lo):
                            last = mm(ps[:, TOK + j // 2, (j % 2) * D:(j % 2 + 1) * D],
                                      part[:, f, j * P:(j + 1) * P], w2q[:, f * D:(f + 1) * D],
                                      f == 0 and part is h_hi, f == NF - 1 and part is h_lo)
                    if j % 2 == 1:
                        last.then_inc(f2_done, 1)

            def slot(k, p):
                b = 2 * k + p
                is_int = isinstance(b, int)
                first, final = is_int and b == 0, is_int and b == NB - 1
                n, kn, pn = b + 1, k + p, 1 - p
                pe.wait_ge(kv_ready, ND * b + ND)
                pe.wait_ge(qt_ready, ND * b + ND)
                for j in range(NJ):
                    for c in range(ND):
                        w = YW // ND
                        last = mm(ps[:, MID + j, c * w:(c + 1) * w], q_t[:, c, j * P:(j + 1) * P],
                                  kv[:, c * HPC:(c + 1) * HPC, :], True, True)
                    last.then_inc(y_done, 1)
                if not final:
                    pe.wait_ge(s_xt[pn], 16 * (kn + 1))
                    if not first:
                        pe.wait_ge(h_ready, NF * b - 2)
                    qk_tile(n, kn, pn, 0)
                    qk_tile(n, kn, pn, 1)
                if not first:
                    pe.wait_ge(h_ready, NF * b)
                pe.wait_ge(y_ready, 2 * b + 2)
                for c in range(ND):
                    for j in range(NJ):
                        last = nc.tensor.transpose(ps[:, TRN + c, j * P:(j + 1) * P],
                                                   y[:, j, c * P:(c + 1) * P], ident[:, :])
                    last.then_inc(yt_done, 1)
                if not final:
                    qk_tile(n, kn, pn, 2)
                if first:
                    pe.wait_ge(s_w["wo"], 16)
                pe.wait_ge(yt_ready, ND * b + ND)
                for j in range(NJ):
                    for c in range(ND):
                        last = mm(ps[:, MID + j // 2, (j % 2) * D:(j % 2 + 1) * D],
                                  y_t[:, c, j * P:(j + 1) * P], wo[:, c, :], c == 0, c == ND - 1)
                    if j % 2 == 1:
                        last.then_inc(o_done, 1)
                if not final:
                    qk_tile(n, kn, pn, 3)
                if not first:
                    ffn2(b - 1)
                pe.wait_ge(x1_ready, NJ * b + NJ)
                for c in range(ND):
                    for j in range(NJ):
                        last = nc.tensor.transpose(ps[:, TRN + c, j * P:(j + 1) * P],
                                                   x1[:, j, c * P:(c + 1) * P], ident[:, :])
                    last.then_inc(x1t_done, 1)
                if not final:
                    g_and_qt(n, kn, pn, False)
                if first:
                    pe.wait_ge(w_quant, 1)
                pe.wait_ge(x1lo_ready, ND * b + ND)
                if not final:
                    pe.wait_ge(qk_added, NJ * n + NJ)
                ffn1(b, range(NF // 2))
                if not final:
                    k_sum_and_kv(n, False)
                ffn1(b, range(NF // 2, NF))

            pe.wait_ge(s_w["wqk"], 16)
            pe.wait_ge(s_xt[0], 16)
            for j in range(NJ):
                qk_tile(0, 0, 0, j)
            g_and_qt(0, 0, 0, True)
            k_sum_and_kv(0, True)
            pe.wait_ge(w_abs, 2)
            pe.wait_ge(qk_added, NJ)
            mm(ps[:, WORK, 0:2], ones[:, :], wsum[:, :], True, True).then_inc(w_total, 1)
            pe.wait_ge(w_thr, 1)
            run_slots(pe, slot)
            ffn2(NB - 1)

        @block.scalar
        def _(act):
            def exp_tile(n, j):
                act.wait_ge(qk_shift, NJ * n + j + 1)
                nc.scalar.activation(qk_exp[:, j, :], qk_pre[:, j % 2, :], ACT.Exp).then_inc(exp_done, 1)

            def gt_and_qt(n, first):
                act.wait_ge(g_done, n + 1)
                if not first:
                    act.wait_ge(kv_done, n)
                nc.scalar.copy(gt[:, :, :], ps[:, MID, :].rearrange("p (c d) -> p c d", c=ND)).then_inc(gt_ready, 1)
                for c in range(ND):
                    act.wait_ge(qt_done, ND * n + c + 1)
                    if not first and c == 0:
                        act.wait_ge(y_done, NJ * n)
                    nc.scalar.copy(q_t[:, c, :], ps[:, TOK + c, :]).then_inc(qt_ready, 1)

            def slot(k, p):
                b = 2 * k + p
                is_int = isinstance(b, int)
                first, final = is_int and b == 0, is_int and b == NB - 1
                n = b + 1
                if not final:
                    act.wait_ge(g_done, n)
                    act.wait_ge(qt_done, ND * n)
                    act.wait_ge(k_paired, n)
                    exp_tile(n, 0)
                if not first:
                    act.wait_ge(o_done, 2 * b)
                for c in range(ND):
                    act.wait_ge(yt_done, ND * b + c + 1)
                    nc.scalar.copy(y_t[:, c, :], ps[:, TRN + c, :]).then_inc(yt_ready, 1)
                if not final:
                    for j in range(1, NJ):
                        exp_tile(n, j)
                if not first:
                    act.wait_ge(f1_done, NF * b)
                for c in range(ND):
                    act.wait_ge(x1t_done, ND * b + c + 1)
                    nc.scalar.copy(x1_hi[:, c, :], ps[:, TRN + c, :]).then_inc(x1hi_ready, 1)
                if not final:
                    gt_and_qt(n, False)
                if first:
                    act.wait_ge(s_w["b1"], 16)
                else:
                    act.wait_ge(f2_done, 2 * b)
                for f in range(NF):
                    act.wait_ge(f1_done, NF * b + f + 1)
                    if not first or f >= NR:
                        act.wait_ge(hlo_ready, NF * b + f - NR + 1)
                    bank, bias = ps[:, F1_BANKS[f % NR], :], b1_col[:, f:f + 1]
                    if f % 2 == 0:
                        nc.scalar.activation(h_hi[:, f, :], bank, ACT.Relu, bias=bias)
                    nc.scalar.activation(h_full[:, f % NR, :], bank, ACT.Relu, bias=bias).then_inc(h_ready, 1)

            for j in range(NJ):
                exp_tile(0, j)
            gt_and_qt(0, True)
            run_slots(act, slot)

        @block.vector
        def _(dve):
            def qk_tile(n, j, first=False):
                pre = qk_pre[:, j % 2, :]
                heads = pre.rearrange("p (h e) -> p h e", e=HD)
                top = qk_max[:, j % 2, :]
                dve.wait_ge(qk_done, NJ * n + j + 1)
                if not first or j >= 2:
                    dve.wait_ge(exp_done, NJ * n + j - 1)
                nc.vector.tensor_tensor(pre, ps[:, WORK + j % 2, :], bqk_rows[:, :], ALU.add).then_inc(qk_added, 1)
                dve.wait_ge(qk_added, NJ * n + j + 1)
                nc.vector.tensor_reduce(top, heads, AX_X, ALU.max).then_inc(qk_maxed, 1)
                dve.wait_ge(qk_maxed, NJ * n + j + 1)
                nc.vector.tensor_tensor(heads, heads, top.unsqueeze(2).to_broadcast([P, 2 * HEADS, HD]),
                                        ALU.subtract).then_inc(qk_shift, 1)

            def kv_finish(n, first):
                dve.wait_ge(kv_done, n + 1)
                nc.vector.tensor_tensor(kv_cut[:, :, 0:HD], ps[:, MID + 1, 0:D].rearrange("p (h e) -> p h e", e=HD),
                                        mask[:, :].unsqueeze(2).to_broadcast([P, HEADS, HD]),
                                        ALU.mult).then_inc(kv_cut_done, 1)
                nc.vector.tensor_copy(k_sum[:, :], ps[:, MID + 1, KS:KS + ND]).then_inc(kv_cut_done, 1)
                dve.wait_ge(kv_cut_done, 2 * n + 2)
                if not first:
                    dve.wait_ge(y_done, NJ * n)
                for c in range(ND):
                    part = slice(c * HPC, (c + 1) * HPC)
                    nc.vector.scalar_tensor_tensor(kv[:, part, :], bv_mask[:, part, :], k_sum[:, c:c + 1],
                                                   kv_cut[:, part, :], ALU.mult, ALU.add).then_inc(kv_ready, 1)

            def row_stats(r, st, st_done):
                for j in range(NJ):
                    nc.vector.bn_stats(st[:, j, :], r[:, j, :]).then_inc(st_done, 1)

            def row_moments(st, mv, ve, mv_done, ve_done, b):
                for j in range(NJ):
                    nc.vector.bn_aggr(mv[:, j, :], st[:, j, :]).then_inc(mv_done, 1)
                dve.wait_ge(mv_done, NJ * b + NJ)
                nc.vector.tensor_scalar(ve[:, :], mv[:, :, 1], LN_EPS, None, ALU.add).then_inc(ve_done, 1)

            def h_low(b, chunks):
                for f in chunks:
                    dve.wait_ge(h_ready, NF * b + f + 1)
                    if f % 2 == 1:
                        nc.vector.tensor_copy(h_hi[:, f, :], h_full[:, f % NR, :]).then_inc(hhi_odd, 1)
                        dve.wait_ge(hhi_odd, NF // 2 * b + f // 2 + 1)
                    nc.vector.tensor_tensor(h_lo[:, f, :], h_full[:, f % NR, :], h_hi[:, f, :].bitcast(F32),
                                            ALU.subtract).then_inc(hlo_ready, 1)

            def residual2(m):
                dve.wait_ge(x1b2_ready, m + 1)
                for t in range(2):
                    dve.wait_ge(f2_done, 2 * m + t + 1)
                    nc.vector.tensor_tensor(r2[:, 2 * t:2 * t + 2, :].rearrange("p j c -> p (j c)"), ps[:, TOK + t, :],
                                            x1_b2[:, 2 * t:2 * t + 2, :].rearrange("p j c -> p (j c)"),
                                            ALU.add).then_inc(r2_done, 1)
                dve.wait_ge(r2_done, 2 * m + 2)
                row_stats(r2, st2, st2_done)

            def normalise2(m, km, pm, early):
                dve.wait_ge(rstd2_done, m + 1)
                if not early:
                    dve.wait_ge(s_out[pm], 16 * km)
                for j in range(NJ):
                    nc.vector.tensor_scalar(res[pm][:, j, :], r2[:, j, :], mv2[:, j, 0:1], rstd2[:, j:j + 1],
                                            ALU.subtract, ALU.mult).then_inc(res_ready, 1)

            def slot(k, p):
                b = 2 * k + p
                is_int = isinstance(b, int)
                first, final = is_int and b == 0, is_int and b == NB - 1
                n = b + 1
                if not first:
                    dve.wait_ge(yt_done, ND * b)
                for t in range(2):
                    tiles = slice(2 * t, 2 * t + 2)
                    banks = ps[:, MID + 2 * t:MID + 2 * t + 2, 0:YW].rearrange("p j (h e) -> p j h e", e=HX)
                    dve.wait_ge(y_done, NJ * b + 2 * t + 2)
                    nc.vector.tensor_scalar(den[:, tiles, :], banks[:, :, :, HD], DEN_EPS, None,
                                            ALU.add).then_inc(den_out, 1)
                    dve.wait_ge(den_out, 2 * b + t + 1)
                    nc.vector.reciprocal(rden[:, tiles, :], den[:, tiles, :]).then_inc(den_inv, 1)
                    dve.wait_ge(den_inv, 2 * b + t + 1)
                    for j in (2 * t, 2 * t + 1):
                        last = nc.vector.tensor_tensor(
                            y[:, j, :].rearrange("p (h e) -> p h e", e=HD), banks[:, j - 2 * t, :, 0:HD],
                            rden[:, j, :].unsqueeze(2).to_broadcast([P, HEADS, HD]), ALU.mult)
                    last.then_inc(y_ready, 1)
                if not final:
                    qk_tile(n, 0)
                    qk_tile(n, 1)
                    qk_tile(n, 2)
                dve.wait_ge(xbo_ready, b + 1)
                for t in range(2):
                    dve.wait_ge(o_done, 2 * b + t + 1)
                    nc.vector.tensor_tensor(r1[:, 2 * t:2 * t + 2, :].rearrange("p j c -> p (j c)"), ps[:, MID + t, :],
                                            x_bo[:, 2 * t:2 * t + 2, :].rearrange("p j c -> p (j c)"),
                                            ALU.add).then_inc(r1_done, 1)
                dve.wait_ge(r1_done, 2 * b + 2)
                row_stats(r1, st1, st1_done)
                dve.wait_ge(st1_done, NJ * b + NJ)
                if not final:
                    qk_tile(n, 3)
                row_moments(st1, mv1, ve1, mv1_done, ve1_done, b)
                dve.wait_ge(rstd1_done, b + 1)
                if not first:
                    dve.wait_ge(x1t_done, ND * b)
                    dve.wait_ge(x1b2_ready, b)
                for j in range(NJ):
                    nc.vector.tensor_scalar(x1[:, j, :], r1[:, j, :], mv1[:, j, 0:1], rstd1[:, j:j + 1],
                                            ALU.subtract, ALU.mult).then_inc(x1_ready, 1)
                if first:
                    quantise(0, w1, w1q)
                if not first:
                    residual2(b - 1)
                    dve.wait_ge(st2_done, NJ * b)
                if not first:
                    dve.wait_ge(f1_done, NF * b)
                for c in range(ND):
                    dve.wait_ge(x1hi_ready, ND * b + c + 1)
                    nc.vector.tensor_tensor(x1_lo[:, c, :], ps[:, TRN + c, :], x1_hi[:, c, :].bitcast(F32),
                                            ALU.subtract).then_inc(x1lo_ready, 1)
                if first:
                    quantise(1, w2, w2q)
                else:
                    row_moments(st2, mv2, ve2, mv2_done, ve2_done, b - 1)
                    dve.wait_ge(f2_done, 2 * b)
                h_low(b, range(NF // 2))
                if not first:
                    normalise2(b - 1, k - 1 + p, 1 - p, is_int and b <= 2)
                if not final:
                    kv_finish(n, False)
                h_low(b, range(NF // 2, NF))

            def weight_sums():
                for i, w in enumerate((w1, w2)):
                    dve.wait_ge(s_w["w1" if i == 0 else "w2"], 16)
                    nc.vector.tensor_reduce(wsum[:, i:i + 1], w[:, :], AX_X, ALU.add,
                                            apply_absolute_value=True).then_inc(w_abs, 1)

            def thresholds():
                dve.wait_ge(w_total, 1)
                nc.vector.tensor_scalar(thr[:, :], ps[:, WORK, 0:2], 1.0 / (D * F), Q_EPS,
                                        ALU.mult, ALU.add).then_inc(w_thr, 1)
                dve.wait_ge(w_thr, 1)
                nc.vector.tensor_scalar(neg_thr[:, :], thr[:, :], -0.5, None, ALU.mult).then_inc(w_thr, 1)
                dve.wait_ge(w_thr, 2)
                nc.vector.tensor_scalar(thr[:, :], thr[:, :], 0.5, None, ALU.mult).then_inc(w_thr, 1)

            def quantise(i, w, wq):
                if i == 0:
                    dve.wait_ge(w_thr, 3)
                else:
                    dve.wait_ge(w_quant, i)
                nc.vector.tensor_scalar(below[:, :], w[:, :], neg_thr[:, i:i + 1], None,
                                        ALU.is_lt).then_inc(w_below, 1)
                dve.wait_ge(w_below, i + 1)
                nc.vector.scalar_tensor_tensor(wq[:, :], w[:, :], thr[:, i:i + 1], below[:, :],
                                               ALU.is_gt, ALU.subtract).then_inc(w_quant, 1)

            dve.wait_ge(s_w["bqk"], 16)
            for j in range(NJ):
                qk_tile(0, j, first=True)
            weight_sums()
            dve.wait_ge(s_w["bv"], 16)
            dve.wait_ge(s_w["mask"], 16)
            dve.wait_ge(const_set, 3)
            mask_b = mask[:, :].unsqueeze(2)
            nc.vector.tensor_tensor(bv_mask[:, :, 0:HD], bv_rows[:, :].rearrange("p (h e) -> p h e", e=HD),
                                    mask_b.to_broadcast([P, HEADS, HD]), ALU.mult).then_inc(bvm_ready, 1)
            nc.vector.tensor_copy(bv_mask[:, :, HD], mask[:, :]).then_inc(bvm_ready, 1)
            dve.wait_ge(bvm_ready, 2)
            kv_finish(0, True)
            thresholds()
            run_slots(dve, slot, peeled=3)
            residual2(NB - 1)
            dve.wait_ge(st2_done, NJ * NB)
            row_moments(st2, mv2, ve2, mv2_done, ve2_done, NB - 1)
            normalise2(NB - 1, NB // 2 - 1, 1, False)

        @block.gpsimd
        def _(pool):
            def xbo(n, kn, pn, first):
                pool.wait_ge(s_x[pn], 16 * (kn + 1))
                if first:
                    pool.wait_ge(s_w["bo"], 16)
                else:
                    pool.wait_ge(r1_done, 2 * n)
                nc.gpsimd.tensor_tensor(x_bo[:, :, :], xs[pn][:, :, :], bo_rows[:, :].unsqueeze(1).to_broadcast([P, NJ, D]),
                                        ALU.add).then_inc(xbo_ready, 1)

            def k_over_tiles(n, first):
                pool.wait_ge(exp_done, NJ * n + NJ)
                nc.gpsimd.tensor_tensor(k_pair[:, :, :], qk_exp[:, 0:2, D:2 * D], qk_exp[:, 2:4, D:2 * D],
                                        ALU.add).then_inc(k_paired, 1)
                pool.wait_ge(k_paired, n + 1)
                if not first:
                    pool.wait_ge(kv_done, n)
                nc.gpsimd.tensor_tensor(k_tok[:, :], k_pair[:, 0, :], k_pair[:, 1, :], ALU.add).then_inc(k_tok_ready, 1)

            def rstd(b, ve, r, ve_done, r_done):
                pool.wait_ge(ve_done, b + 1)
                nc.gpsimd.tensor_tensor(r[:, :], ve[:, :], minus_half[:, :], ALU.pow).then_inc(r_done, 1)

            def slot(k, p):
                b = 2 * k + p
                is_int = isinstance(b, int)
                first, final = is_int and b == 0, is_int and b == NB - 1
                rstd(b, ve1, rstd1, ve1_done, rstd1_done)
                if not final:
                    k_over_tiles(b + 1, False)
                if not first:
                    rstd(b - 1, ve2, rstd2, ve2_done, rstd2_done)
                pool.wait_ge(x1_ready, NJ * b + NJ)
                if first:
                    pool.wait_ge(s_w["b2"], 16)
                else:
                    pool.wait_ge(r2_done, 2 * b)
                nc.gpsimd.tensor_tensor(x1_b2[:, :, :], x1[:, :, :], b2_rows[:, :].unsqueeze(1).to_broadcast([P, NJ, D]),
                                        ALU.add).then_inc(x1b2_ready, 1)
                if not final:
                    xbo(b + 1, k + p, 1 - p, False)

            nc.gpsimd.memset(ones[:, :], 1.0).then_inc(const_set, 1)
            nc.gpsimd.memset(minus_half[:, :], -0.5).then_inc(const_set, 1)
            nc.gpsimd.memset(kv_cut[:, :, :], 0.0).then_inc(const_set, 1)
            k_over_tiles(0, True)
            xbo(0, 0, 0, True)
            pool.wait_ge(const_set, 3)
            run_slots(pool, slot)
            rstd(NB - 1, ve2, rstd2, ve2_done, rstd2_done)


def kernel(**inputs):
    import concourse.bacc as bacc
    from concourse.bass_utils import run_bass_kernel_spmd

    a = {n: np.asarray(v) for n, v in inputs.items()}
    x = a["L0_attn_x"]
    nb, s, d = x.shape
    f = a["L0_ffn_b1"].shape[0]
    nj = s // P
    row = lambda v: v.reshape(1, -1)
    heads_of = np.arange(P)[:, None] // (d // 16) == np.arange(P // (d // 16))[None, :]
    arrays = {
        "x": x,
        "x_t": x.reshape(nb, P, nj, d).transpose(0, 3, 2, 1).reshape(nb, d, s),
        "wqk_t": np.concatenate([a["L0_attn_Wq"].T, a["L0_attn_Wk"].T], axis=1),
        "bqk": row(np.concatenate([a["L0_attn_bq"], a["L0_attn_bk"]])),
        "wv_t": a["L0_attn_Wv"].T,
        "bv": row(a["L0_attn_bv"]),
        "wo_t": a["L0_attn_Wo"].T,
        "bo": row(a["L0_attn_bo"]),
        "w1_t": a["L0_ffn_W1"].T,
        "b1": a["L0_ffn_b1"].reshape(f // P, P).T,
        "w2_t": a["L0_ffn_W2"].T,
        "b2": row(a["L0_ffn_b2"]),
        "ident_c": np.eye(P, dtype=np.float32),
        "mask_c": np.tile(heads_of, (1, d // P)).astype(np.float32),
    }
    arrays = {n: np.ascontiguousarray(v) for n, v in arrays.items()}
    nc = bacc.Bacc("TRN2", target_bir_lowering=False, num_devices=1)
    aps = [nc.dram_tensor(n, v.shape, mybir.dt.from_np(v.dtype), kind="ExternalInput").ap() for n, v in arrays.items()]
    out = nc.dram_tensor("out", (nb, s, d), F32, kind="ExternalOutput").ap()
    attention_ffn_block(nc, *aps, out)
    r = run_bass_kernel_spmd(nc, [arrays], core_ids=[0])
    return r.results[0]["out"]
```

```python
from contextlib import ExitStack

import numpy as np

import concourse.bass as bass
from concourse import mybir

F32 = mybir.dt.float32
F32R = mybir.dt.float32r
ALU = mybir.AluOpType
ACT = mybir.ActivationFunctionType
AX_X = mybir.AxisListType.X

P = 128
LN_EPS = 1e-5
Q_EPS = 1e-5
DEN_EPS = 1e-6


def attention_ffn_block(nc, x, x_t, wqk_t, bqk, wv_t, bv, wo_t, bo, w1_t, b1, w2_t, b2, ident_c, mask_c, out):
    NB, S, D = x.shape
    F = w1_t.shape[1]
    HEADS = 16
    HD = D // HEADS
    NJ = S // P
    ND = D // P
    NF = F // P
    NR = 4
    assert NJ == 4 and ND == 2 and NB % 2 == 0 and NB >= 4

    with ExitStack() as ctx:
        def sb(name, shape, dt=F32):
            return ctx.enter_context(nc.sbuf_tensor(name, shape, dt))

        def sem(name):
            return ctx.enter_context(nc.semaphore(name))

        wqk = sb("wqk", [P, ND, 2 * D])
        wv = sb("wv", [P, ND, D])
        wo = sb("wo", [P, ND, D])
        w1 = sb("w1", [P, ND * F])
        w2 = sb("w2", [P, NF * D])
        w1q = sb("w1q", [P, ND * F], F32R)
        w2q = sb("w2q", [P, NF * D], F32R)
        below = sb("below", [P, ND * F])
        bqk_rows = sb("bqk_rows", [P, 2 * D])
        bo_rows = sb("bo_rows", [P, D])
        b2_rows = sb("b2_rows", [P, D])
        bv_col = sb("bv_col", [P, ND])
        b1_col = sb("b1_col", [P, NF])
        ident = sb("ident", [P, P])
        mask = sb("mask", [P, HEADS])
        ones = sb("ones", [P, P])
        minus_half = sb("minus_half", [P, NJ])
        wsum = sb("wsum", [P, 2])
        thr = sb("thr", [P, 2])
        neg_thr = sb("neg_thr", [P, 2])

        xs = [sb(f"xs{p}", [P, NJ, D]) for p in range(2)]
        xt = [sb(f"xt{p}", [P, ND, S]) for p in range(2)]
        x_bo = sb("x_bo", [P, NJ, D])
        qk_pre = sb("qk_pre", [P, 2, 2 * D])
        qk_max = sb("qk_max", [P, 2, 2 * HEADS])
        qk_exp = sb("qk_exp", [P, NJ, 2 * D])
        k_pair = sb("k_pair", [P, 2, D])
        k_tok = sb("k_tok", [P, D])
        gt = sb("gt", [P, ND, D])
        k_sum = sb("k_sum", [P, D])
        qk_sum = sb("qk_sum", [P, NJ, D])
        den = sb("den", [P, NJ, HEADS])
        den_eps = sb("den_eps", [P, NJ, HEADS])
        rden = sb("rden", [P, NJ, HEADS])
        kv_raw = sb("kv_raw", [P, D])
        kv_t = sb("kv_t", [P, D])
        m = sb("m", [P, ND, D])
        q_t = sb("q_t", [P, ND, S])
        r1 = sb("r1", [P, NJ, D])
        st1 = sb("st1", [P, NJ, 6])
        mv1 = sb("mv1", [P, NJ, 2])
        ve1 = sb("ve1", [P, NJ])
        rstd1 = sb("rstd1", [P, NJ])
        shift1 = sb("shift1", [P, NJ])
        x1 = sb("x1", [P, NJ, D])
        x1_b2 = sb("x1_b2", [P, NJ, D])
        x1_hi = sb("x1_hi", [P, ND, S], F32R)
        x1_lo = sb("x1_lo", [P, ND, S], F32R)
        h_full = sb("h_full", [P, NR, S])
        h_hi = sb("h_hi", [P, NF, S], F32R)
        h_lo = sb("h_lo", [P, NF, S], F32R)
        r2 = sb("r2", [P, NJ, D])
        st2 = sb("st2", [P, NJ, 6])
        mv2 = sb("mv2", [P, NJ, 2])
        ve2 = sb("ve2", [P, NJ])
        rstd2 = sb("rstd2", [P, NJ])
        shift2 = sb("shift2", [P, NJ])
        res = [sb(f"res{p}", [P, NJ, D]) for p in range(2)]

        ps = ctx.enter_context(nc.psum_tensor("ps", [P, 8, 512], F32))
        WORK = 0
        MID = 2
        TOK = 4
        TRN = 6
        F1_BANKS = (WORK, WORK + 1, TRN, TRN + 1)
        s_w = {n: sem(f"s_{n}") for n in ("wqk", "bqk", "wv", "ident", "mask", "bv", "bo", "wo", "w1", "w2", "b1", "b2")}
        s_x = [sem(f"s_x{p}") for p in range(2)]
        s_xt = [sem(f"s_xt{p}") for p in range(2)]
        s_out = [sem(f"s_out{p}") for p in range(2)]
        const_set = sem("const_set")
        w_abs = sem("w_abs")
        w_total = sem("w_total")
        w_thr = sem("w_thr")
        w_below = sem("w_below")
        w_quant = sem("w_quant")
        qk_done = sem("qk_done")
        qk_added = sem("qk_added")
        qk_maxed = sem("qk_maxed")
        qk_shift = sem("qk_shift")
        exp_done = sem("exp_done")
        g_done = sem("g_done")
        gt_ready = sem("gt_ready")
        qt_done = sem("qt_done")
        qt_ready = sem("qt_ready")
        k_paired = sem("k_paired")
        k_tok_ready = sem("k_tok_ready")
        ksum_done = sem("ksum_done")
        ksum_ready = sem("ksum_ready")
        q_times_ksum = sem("q_times_ksum")
        den_ready = sem("den_ready")
        q_ready = sem("q_ready")
        kv_done = sem("kv_done")
        kv_biased = sem("kv_biased")
        kv_ready = sem("kv_ready")
        m_done = sem("m_done")
        m_ready = sem("m_ready")
        o_done = sem("o_done")
        xbo_ready = sem("xbo_ready")
        r1_done = sem("r1_done")
        st1_done = sem("st1_done")
        mv1_done = sem("mv1_done")
        ve1_done = sem("ve1_done")
        rstd1_done = sem("rstd1_done")
        shift1_done = sem("shift1_done")
        x1_ready = sem("x1_ready")
        x1b2_ready = sem("x1b2_ready")
        x1t_done = sem("x1t_done")
        x1hi_ready = sem("x1hi_ready")
        x1lo_ready = sem("x1lo_ready")
        f1_done = sem("f1_done")
        h_ready = sem("h_ready")
        hhi_odd = sem("hhi_odd")
        hlo_ready = sem("hlo_ready")
        f2_done = sem("f2_done")
        r2_done = sem("r2_done")
        st2_done = sem("st2_done")
        mv2_done = sem("mv2_done")
        ve2_done = sem("ve2_done")
        rstd2_done = sem("rstd2_done")
        shift2_done = sem("shift2_done")
        res_ready = sem("res_ready")

        def run_slots(eng, slot, peeled=1, last_looped=NB - 2):
            for b in range(peeled):
                slot(b // 2, b % 2)
            with eng.Fori(peeled // 2, last_looped // 2) as k:
                slot(k, 1)
                slot(k + 1, 0)
            for b in range(last_looped + 1, NB):
                slot(b // 2, b % 2)

        block = ctx.enter_context(nc.Block())

        @block.sync
        def _(sp):
            def load(b, k, p):
                sp.dma_start(xt[p][:, :, :], x_t[b].rearrange("(c p) t -> p c t", p=P)).then_inc(s_xt[p], 16)
                sp.dma_start(xs[p][:, :, :], x[b].rearrange("(p j) c -> p j c", j=NJ)).then_inc(s_x[p], 16)

            def weight(name, dst, src):
                sp.dma_start(dst, src).then_inc(s_w[name], 16)

            weight("wqk", wqk[:, :, :], wqk_t.rearrange("(c p) n -> p c n", p=P))
            load(0, 0, 0)
            weight("bqk", bqk_rows[:, :], bqk.to_broadcast([P, 2 * D]))
            weight("w1", w1[:, :].rearrange("p (c n) -> p c n", c=ND), w1_t.rearrange("(c p) n -> p c n", p=P))
            weight("w2", w2[:, :].rearrange("p (c n) -> p c n", c=NF), w2_t.rearrange("(c p) n -> p c n", p=P))
            weight("ident", ident[:, :], ident_c)
            weight("mask", mask[:, :], mask_c)
            weight("bv", bv_col[:, :], bv)
            weight("wv", wv[:, :, :], wv_t.rearrange("(c p) n -> p c n", p=P))
            weight("bo", bo_rows[:, :], bo.to_broadcast([P, D]))
            weight("wo", wo[:, :, :], wo_t.rearrange("(c p) n -> p c n", p=P))
            weight("b1", b1_col[:, :], b1)
            weight("b2", b2_rows[:, :], b2.to_broadcast([P, D]))
            load(1, 0, 1)

            def store(m, k, p):
                sp.wait_ge(res_ready, NJ * m + NJ)
                sp.dma_start(out[m].rearrange("(p j) c -> p j c", j=NJ), res[p][:, :, :]).then_inc(s_out[p], 16)

            def slot(k, p):
                b = 2 * k + p
                looped = not isinstance(b, int)
                if looped or b + 2 < NB:
                    sp.wait_ge(g_done, b + 1)
                    sp.wait_ge(xbo_ready, b + 1)
                    sp.wait_ge(qk_done, NJ * b + NJ)
                    load(b + 2, k + 1, p)
                if looped or b > 0:
                    store(b - 1, k - 1 + p, 1 - p)

            run_slots(sp, slot, last_looped=NB - 4)
            store(NB - 1, NB // 2 - 1, 1)
            for p in range(2):
                sp.wait_ge(s_out[p], 16 * (NB // 2))

        @block.tensor
        def _(pe):
            def mm(dst, lhs, rhs, start, stop):
                return nc.tensor.matmul(dst, lhs, rhs, start=start, stop=stop)

            def qk_tile(n, kn, pn, j):
                bank = ps[:, WORK + j % 2, :]
                if j >= 2:
                    pe.wait_ge(qk_added, NJ * n + j - 1)
                for c in range(ND):
                    last = mm(bank, xt[pn][:, c, j * P:(j + 1) * P], wqk[:, c, :], c == 0, c == ND - 1)
                last.then_inc(qk_done, 1)

            def k_total(n, first):
                pe.wait_ge(k_tok_ready, n + 1)
                if first:
                    pe.wait_ge(const_set, 2)
                else:
                    pe.wait_ge(r1_done, 2 * n)
                mm(ps[:, MID + 1, 0:D], ones[:, :], k_tok[:, :], True, True).then_inc(ksum_done, 1)

            def g_product(n, kn, pn):
                pe.wait_ge(exp_done, NJ * n + NJ)
                pe.wait_ge(s_x[pn], 16 * (kn + 1))
                for c in range(ND):
                    for j in range(NJ):
                        last = mm(ps[:, MID, c * D:(c + 1) * D], xs[pn][:, j, c * P:(c + 1) * P],
                                  qk_exp[:, j, D:2 * D], j == 0, j == NJ - 1)
                last.then_inc(g_done, 1)

            def kv_product(n):
                pe.wait_ge(ksum_ready, n + 1)
                pe.wait_ge(gt_ready, n + 1)
                for h in range(ND):
                    for c in range(ND):
                        last = mm(ps[:, MID + 1, h * P:(h + 1) * P], wv[:, c, h * P:(h + 1) * P],
                                  gt[:, c, h * P:(h + 1) * P], c == 0, c == ND - 1)
                last.then_inc(kv_done, 1)

            def m_product(n):
                pe.wait_ge(kv_ready, n + 1)
                for h in range(ND):
                    last = mm(ps[:, MID, h * D:(h + 1) * D], kv_t[:, h * P:(h + 1) * P], wo[:, h, :], True, True)
                last.then_inc(m_done, 1)

            def q_transpose(n, free):
                if not free:
                    pe.wait_ge(r2_done, 2 * n - 2)
                pe.wait_ge(q_ready, n + 1)
                for c in range(ND):
                    for j in range(NJ):
                        last = nc.tensor.transpose(ps[:, TOK + c, j * P:(j + 1) * P],
                                                   qk_exp[:, j, c * P:(c + 1) * P], ident[:, :])
                    last.then_inc(qt_done, 1)

            def ffn1(b, chunks):
                for f in chunks:
                    if f >= NR:
                        pe.wait_ge(h_ready, NF * b + f - NR + 1)
                    for c in range(ND):
                        for part in (x1_hi, x1_lo):
                            last = mm(ps[:, F1_BANKS[f % NR], :], w1q[:, c * F + f * P:c * F + (f + 1) * P],
                                      part[:, c, :], c == 0 and part is x1_hi, c == ND - 1 and part is x1_lo)
                    last.then_inc(f1_done, 1)

            def ffn2(m):
                pe.wait_ge(hlo_ready, NF * m + NF)
                for j in range(NJ):
                    for f in range(NF):
                        for part in (h_hi, h_lo):
                            last = mm(ps[:, TOK + j // 2, (j % 2) * D:(j % 2 + 1) * D],
                                      part[:, f, j * P:(j + 1) * P], w2q[:, f * D:(f + 1) * D],
                                      f == 0 and part is h_hi, f == NF - 1 and part is h_lo)
                    if j % 2 == 1:
                        last.then_inc(f2_done, 1)

            def slot(k, p):
                b = 2 * k + p
                is_int = isinstance(b, int)
                first, final = is_int and b == 0, is_int and b == NB - 1
                n, kn, pn = b + 1, k + p, 1 - p
                if not final:
                    pe.wait_ge(s_xt[pn], 16 * (kn + 1))
                    if not first:
                        pe.wait_ge(h_ready, NF * b - 2)
                    qk_tile(n, kn, pn, 0)
                    qk_tile(n, kn, pn, 1)
                if first:
                    pe.wait_ge(s_w["wo"], 16)
                    m_product(0)
                    pe.wait_ge(s_w["ident"], 16)
                    q_transpose(0, True)
                pe.wait_ge(m_ready, b + 1)
                pe.wait_ge(kv_biased, ND * b + ND)
                pe.wait_ge(qt_ready, ND * b + ND)
                for j in range(NJ):
                    for c in range(ND):
                        last = mm(ps[:, MID + j // 2, (j % 2) * D:(j % 2 + 1) * D],
                                  q_t[:, c, j * P:(j + 1) * P], m[:, c, :], c == 0, c == ND - 1)
                    if j % 2 == 1:
                        last.then_inc(o_done, 1)
                if not final:
                    qk_tile(n, kn, pn, 2)
                    qk_tile(n, kn, pn, 3)
                if not first:
                    ffn2(b - 1)
                if not final:
                    k_total(n, False)
                pe.wait_ge(x1_ready, NJ * b + NJ)
                if not first:
                    pe.wait_ge(h_ready, NF * b)
                for c in range(ND):
                    for j in range(NJ):
                        last = nc.tensor.transpose(ps[:, TRN + c, j * P:(j + 1) * P],
                                                   x1[:, j, c * P:(c + 1) * P], ident[:, :])
                    last.then_inc(x1t_done, 1)
                if not final:
                    g_product(n, kn, pn)
                if first:
                    pe.wait_ge(w_quant, 1)
                pe.wait_ge(x1lo_ready, ND * b + ND)
                if not final:
                    pe.wait_ge(qk_added, NJ * n + NJ)
                ffn1(b, range(NF // 2))
                if not final:
                    kv_product(n)
                ffn1(b, range(NF // 2, 3 * NF // 4))
                if not final:
                    m_product(n)
                    q_transpose(n, first)
                ffn1(b, range(3 * NF // 4, NF))

            pe.wait_ge(s_w["wqk"], 16)
            pe.wait_ge(s_xt[0], 16)
            for j in range(NJ):
                qk_tile(0, 0, 0, j)
            k_total(0, True)
            g_product(0, 0, 0)
            pe.wait_ge(s_w["wv"], 16)
            kv_product(0)
            pe.wait_ge(w_abs, 2)
            pe.wait_ge(qk_added, NJ)
            mm(ps[:, WORK, 0:2], ones[:, :], wsum[:, :], True, True).then_inc(w_total, 1)
            pe.wait_ge(w_thr, 1)
            run_slots(pe, slot)
            ffn2(NB - 1)

        @block.scalar
        def _(act):
            def exp_tile(n, j):
                act.wait_ge(qk_shift, NJ * n + j + 1)
                nc.scalar.activation(qk_exp[:, j, :], qk_pre[:, j % 2, :], ACT.Exp).then_inc(exp_done, 1)

            def m_and_qt(n, first):
                act.wait_ge(m_done, n + 1)
                if not first:
                    act.wait_ge(o_done, 2 * n)
                nc.scalar.copy(m[:, :, :], ps[:, MID, :].rearrange("p (c d) -> p c d", c=ND)).then_inc(m_ready, 1)
                for c in range(ND):
                    act.wait_ge(qt_done, ND * n + c + 1)
                    nc.scalar.copy(q_t[:, c, :], ps[:, TOK + c, :]).then_inc(qt_ready, 1)

            def k_sum_out(n, first):
                act.wait_ge(ksum_done, n + 1)
                if not first:
                    act.wait_ge(kv_biased, ND * n)
                nc.scalar.copy(k_sum[:, :], ps[:, MID + 1, 0:D]).then_inc(ksum_ready, 1)

            def gt_out(n, first):
                act.wait_ge(g_done, n + 1)
                if not first:
                    act.wait_ge(kv_done, n)
                nc.scalar.copy(gt[:, :, :], ps[:, MID, :].rearrange("p (c d) -> p c d", c=ND)).then_inc(gt_ready, 1)

            def normalise(dst, r, rstd, shift, ready):
                for j in range(NJ):
                    nc.scalar.activation(dst[:, j, :], r[:, j, :], ACT.Identity, scale=rstd[:, j:j + 1],
                                         bias=shift[:, j:j + 1]).then_inc(ready, 1)

            def normalise2(mb, km, pm, early):
                act.wait_ge(shift2_done, mb + 1)
                if not early:
                    act.wait_ge(s_out[pm], 16 * km)
                normalise(res[pm], r2, rstd2, shift2, res_ready)

            def hidden(b, first, chunks):
                for f in chunks:
                    act.wait_ge(f1_done, NF * b + f + 1)
                    if not first or f >= NR:
                        act.wait_ge(hlo_ready, NF * b + f - NR + 1)
                    bank, bias = ps[:, F1_BANKS[f % NR], :], b1_col[:, f:f + 1]
                    if f % 2 == 0:
                        nc.scalar.activation(h_hi[:, f, :], bank, ACT.Relu, bias=bias)
                    nc.scalar.activation(h_full[:, f % NR, :], bank, ACT.Relu, bias=bias).then_inc(h_ready, 1)

            def slot(k, p):
                b = 2 * k + p
                is_int = isinstance(b, int)
                first, final = is_int and b == 0, is_int and b == NB - 1
                n = b + 1
                if first:
                    m_and_qt(0, True)
                if not final:
                    act.wait_ge(g_done, n)
                    act.wait_ge(qt_done, ND * n)
                    act.wait_ge(k_paired, n)
                    for j in range(3):
                        exp_tile(n, j)
                act.wait_ge(shift1_done, b + 1)
                if not first:
                    act.wait_ge(x1t_done, ND * b)
                    act.wait_ge(x1b2_ready, b)
                normalise(x1, r1, rstd1, shift1, x1_ready)
                if not final:
                    exp_tile(n, 3)
                    k_sum_out(n, False)
                if not first:
                    act.wait_ge(f1_done, NF * b)
                for c in range(ND):
                    act.wait_ge(x1t_done, ND * b + c + 1)
                    nc.scalar.copy(x1_hi[:, c, :], ps[:, TRN + c, :]).then_inc(x1hi_ready, 1)
                if not final:
                    gt_out(n, False)
                if first:
                    act.wait_ge(s_w["b1"], 16)
                else:
                    act.wait_ge(f2_done, 2 * b)
                hidden(b, first, range(2))
                if not first:
                    normalise2(b - 1, k - 1 + p, 1 - p, is_int and b <= 2)
                hidden(b, first, range(2, 3 * NF // 4))
                if not final:
                    m_and_qt(n, False)
                hidden(b, first, range(3 * NF // 4, NF))

            for j in range(NJ):
                exp_tile(0, j)
            k_sum_out(0, True)
            gt_out(0, True)
            run_slots(act, slot, peeled=3)
            normalise2(NB - 1, NB // 2 - 1, 1, False)

        @block.vector
        def _(dve):
            def qk_add(n, j, first=False):
                dve.wait_ge(qk_done, NJ * n + j + 1)
                if not first or j >= 2:
                    dve.wait_ge(exp_done, NJ * n + j - 1)
                nc.vector.tensor_tensor(qk_pre[:, j % 2, :], ps[:, WORK + j % 2, :], bqk_rows[:, :],
                                        ALU.add).then_inc(qk_added, 1)

            def qk_less_max(n, j):
                heads = qk_pre[:, j % 2, :].rearrange("p (h e) -> p h e", e=HD)
                top = qk_max[:, j % 2, :]
                dve.wait_ge(qk_added, NJ * n + j + 1)
                nc.vector.tensor_reduce(top, heads, AX_X, ALU.max).then_inc(qk_maxed, 1)
                dve.wait_ge(qk_maxed, NJ * n + j + 1)
                nc.vector.tensor_tensor(heads, heads, top.unsqueeze(2).to_broadcast([P, 2 * HEADS, HD]),
                                        ALU.subtract).then_inc(qk_shift, 1)

            def q_normalise(n):
                q = qk_exp[:, :, 0:D]
                dve.wait_ge(exp_done, NJ * n + NJ)
                dve.wait_ge(ksum_ready, n + 1)
                nc.vector.tensor_tensor(qk_sum[:, :, :], q, k_sum[:, :].unsqueeze(1).to_broadcast([P, NJ, D]),
                                        ALU.mult).then_inc(q_times_ksum, 1)
                dve.wait_ge(q_times_ksum, n + 1)
                nc.vector.tensor_reduce(den[:, :, :].rearrange("p j h -> p (j h)"),
                                        qk_sum[:, :, :].rearrange("p j (h e) -> p (j h) e", e=HD), AX_X,
                                        ALU.add).then_inc(den_ready, 1)
                dve.wait_ge(den_ready, 3 * n + 1)
                nc.vector.tensor_scalar(den_eps[:, :, :], den[:, :, :], DEN_EPS, None, ALU.add).then_inc(den_ready, 1)
                dve.wait_ge(den_ready, 3 * n + 2)
                nc.vector.reciprocal(rden[:, :, :], den_eps[:, :, :]).then_inc(den_ready, 1)
                dve.wait_ge(den_ready, 3 * n + 3)
                for j in range(NJ):
                    q_heads = q[:, j, :].rearrange("p (h e) -> p h e", e=HD)
                    last = nc.vector.tensor_tensor(q_heads, q_heads,
                                                   rden[:, j, :].unsqueeze(2).to_broadcast([P, HEADS, HD]), ALU.mult)
                last.then_inc(q_ready, 1)

            def kv_finish(n, first):
                dve.wait_ge(kv_done, n + 1)
                for h in range(ND):
                    d = slice(h * P, (h + 1) * P)
                    nc.vector.scalar_tensor_tensor(kv_raw[:, d], k_sum[:, d], bv_col[:, h:h + 1], ps[:, MID + 1, d],
                                                   ALU.mult, ALU.add).then_inc(kv_biased, 1)
                if not first:
                    dve.wait_ge(m_done, n)
                dve.wait_ge(kv_biased, ND * n + ND)
                nc.vector.tensor_tensor(kv_t[:, :].rearrange("p (h e) -> p h e", e=HD),
                                        kv_raw[:, :].rearrange("p (h e) -> p h e", e=HD),
                                        mask[:, :].unsqueeze(2).to_broadcast([P, HEADS, HD]),
                                        ALU.mult).then_inc(kv_ready, 1)

            def row_stats(r, st, st_done):
                for j in range(NJ):
                    nc.vector.bn_stats(st[:, j, :], r[:, j, :]).then_inc(st_done, 1)

            def row_moments(st, mv, ve, mv_done, ve_done, b):
                for j in range(NJ):
                    nc.vector.bn_aggr(mv[:, j, :], st[:, j, :]).then_inc(mv_done, 1)
                dve.wait_ge(mv_done, NJ * b + NJ)
                nc.vector.tensor_scalar(ve[:, :], mv[:, :, 1], LN_EPS, None, ALU.add).then_inc(ve_done, 1)

            def h_low(b, chunks):
                for f in chunks:
                    dve.wait_ge(h_ready, NF * b + f + 1)
                    if f % 2 == 1:
                        nc.vector.tensor_copy(h_hi[:, f, :], h_full[:, f % NR, :]).then_inc(hhi_odd, 1)
                        dve.wait_ge(hhi_odd, NF // 2 * b + f // 2 + 1)
                    nc.vector.tensor_tensor(h_lo[:, f, :], h_full[:, f % NR, :], h_hi[:, f, :].bitcast(F32),
                                            ALU.subtract).then_inc(hlo_ready, 1)

            def residual2(m):
                dve.wait_ge(x1b2_ready, m + 1)
                if not isinstance(m, int) or m > 0:
                    dve.wait_ge(res_ready, NJ * m)
                for t in range(2):
                    dve.wait_ge(f2_done, 2 * m + t + 1)
                    nc.vector.tensor_tensor(r2[:, 2 * t:2 * t + 2, :].rearrange("p j c -> p (j c)"), ps[:, TOK + t, :],
                                            x1_b2[:, 2 * t:2 * t + 2, :].rearrange("p j c -> p (j c)"),
                                            ALU.add).then_inc(r2_done, 1)
                dve.wait_ge(r2_done, 2 * m + 2)
                row_stats(r2, st2, st2_done)

            def shift(mv, rstd, sh, rstd_done, sh_done, b):
                dve.wait_ge(rstd_done, b + 1)
                nc.vector.scalar_tensor_tensor(sh[:, :], mv[:, :, 0], -1.0, rstd[:, :], ALU.mult,
                                               ALU.mult).then_inc(sh_done, 1)

            def slot(k, p):
                b = 2 * k + p
                is_int = isinstance(b, int)
                first, final = is_int and b == 0, is_int and b == NB - 1
                n = b + 1
                if not final:
                    for j in range(2):
                        qk_add(n, j)
                        qk_less_max(n, j)
                dve.wait_ge(xbo_ready, b + 1)
                if not first:
                    dve.wait_ge(x1_ready, NJ * b)
                for t in range(2):
                    dve.wait_ge(o_done, 2 * b + t + 1)
                    nc.vector.tensor_tensor(r1[:, 2 * t:2 * t + 2, :].rearrange("p j c -> p (j c)"), ps[:, MID + t, :],
                                            x_bo[:, 2 * t:2 * t + 2, :].rearrange("p j c -> p (j c)"),
                                            ALU.add).then_inc(r1_done, 1)
                dve.wait_ge(r1_done, 2 * b + 2)
                row_stats(r1, st1, st1_done)
                dve.wait_ge(st1_done, NJ * b + NJ)
                if not final:
                    qk_add(n, 2)
                row_moments(st1, mv1, ve1, mv1_done, ve1_done, b)
                if not final:
                    qk_less_max(n, 2)
                    shift(mv1, rstd1, shift1, rstd1_done, shift1_done, b)
                    qk_add(n, 3)
                    qk_less_max(n, 3)
                else:
                    shift(mv1, rstd1, shift1, rstd1_done, shift1_done, b)
                if first:
                    quantise(0, w1, w1q)
                else:
                    residual2(b - 1)
                    dve.wait_ge(st2_done, NJ * b)
                if not first:
                    dve.wait_ge(f1_done, NF * b)
                for c in range(ND):
                    dve.wait_ge(x1hi_ready, ND * b + c + 1)
                    nc.vector.tensor_tensor(x1_lo[:, c, :], ps[:, TRN + c, :], x1_hi[:, c, :].bitcast(F32),
                                            ALU.subtract).then_inc(x1lo_ready, 1)
                if not first:
                    row_moments(st2, mv2, ve2, mv2_done, ve2_done, b - 1)
                if not final:
                    q_normalise(n)
                if first:
                    quantise(1, w2, w2q)
                else:
                    shift(mv2, rstd2, shift2, rstd2_done, shift2_done, b - 1)
                    dve.wait_ge(f2_done, 2 * b)
                h_low(b, range(2))
                if not final:
                    kv_finish(n, False)
                h_low(b, range(2, NF))

            def weight_sums():
                for i, w in enumerate((w1, w2)):
                    dve.wait_ge(s_w["w1" if i == 0 else "w2"], 16)
                    nc.vector.tensor_reduce(wsum[:, i:i + 1], w[:, :], AX_X, ALU.add,
                                            apply_absolute_value=True).then_inc(w_abs, 1)

            def thresholds():
                dve.wait_ge(w_total, 1)
                nc.vector.tensor_scalar(thr[:, :], ps[:, WORK, 0:2], 1.0 / (D * F), Q_EPS,
                                        ALU.mult, ALU.add).then_inc(w_thr, 1)
                dve.wait_ge(w_thr, 1)
                nc.vector.tensor_scalar(neg_thr[:, :], thr[:, :], -0.5, None, ALU.mult).then_inc(w_thr, 1)
                dve.wait_ge(w_thr, 2)
                nc.vector.tensor_scalar(thr[:, :], thr[:, :], 0.5, None, ALU.mult).then_inc(w_thr, 1)

            def quantise(i, w, wq):
                if i == 0:
                    dve.wait_ge(w_thr, 3)
                else:
                    dve.wait_ge(w_quant, i)
                nc.vector.tensor_scalar(below[:, :], w[:, :], neg_thr[:, i:i + 1], None,
                                        ALU.is_lt).then_inc(w_below, 1)
                dve.wait_ge(w_below, i + 1)
                nc.vector.scalar_tensor_tensor(wq[:, :], w[:, :], thr[:, i:i + 1], below[:, :],
                                               ALU.is_gt, ALU.subtract).then_inc(w_quant, 1)

            dve.wait_ge(s_w["bqk"], 16)
            for j in range(NJ):
                qk_add(0, j, first=True)
                qk_less_max(0, j)
            weight_sums()
            q_normalise(0)
            dve.wait_ge(s_w["bv"], 16)
            dve.wait_ge(s_w["mask"], 16)
            kv_finish(0, True)
            thresholds()
            run_slots(dve, slot)
            residual2(NB - 1)
            dve.wait_ge(st2_done, NJ * NB)
            row_moments(st2, mv2, ve2, mv2_done, ve2_done, NB - 1)
            shift(mv2, rstd2, shift2, rstd2_done, shift2_done, NB - 1)

        @block.gpsimd
        def _(pool):
            def xbo(n, kn, pn, first):
                pool.wait_ge(s_x[pn], 16 * (kn + 1))
                if first:
                    pool.wait_ge(s_w["bo"], 16)
                else:
                    pool.wait_ge(r1_done, 2 * n)
                nc.gpsimd.tensor_tensor(x_bo[:, :, :], xs[pn][:, :, :], bo_rows[:, :].unsqueeze(1).to_broadcast([P, NJ, D]),
                                        ALU.add).then_inc(xbo_ready, 1)

            def k_over_tiles(n, first):
                pool.wait_ge(exp_done, NJ * n + NJ)
                nc.gpsimd.tensor_tensor(k_pair[:, :, :], qk_exp[:, 0:2, D:2 * D], qk_exp[:, 2:4, D:2 * D],
                                        ALU.add).then_inc(k_paired, 1)
                pool.wait_ge(k_paired, n + 1)
                if not first:
                    pool.wait_ge(ksum_done, n)
                nc.gpsimd.tensor_tensor(k_tok[:, :], k_pair[:, 0, :], k_pair[:, 1, :], ALU.add).then_inc(k_tok_ready, 1)

            def rstd(b, ve, r, ve_done, r_done):
                pool.wait_ge(ve_done, b + 1)
                nc.gpsimd.tensor_tensor(r[:, :], ve[:, :], minus_half[:, :], ALU.pow).then_inc(r_done, 1)

            def slot(k, p):
                b = 2 * k + p
                is_int = isinstance(b, int)
                first, final = is_int and b == 0, is_int and b == NB - 1
                rstd(b, ve1, rstd1, ve1_done, rstd1_done)
                if not final:
                    k_over_tiles(b + 1, False)
                if not first:
                    rstd(b - 1, ve2, rstd2, ve2_done, rstd2_done)
                pool.wait_ge(x1_ready, NJ * b + NJ)
                if first:
                    pool.wait_ge(s_w["b2"], 16)
                else:
                    pool.wait_ge(r2_done, 2 * b)
                nc.gpsimd.tensor_tensor(x1_b2[:, :, :], x1[:, :, :], b2_rows[:, :].unsqueeze(1).to_broadcast([P, NJ, D]),
                                        ALU.add).then_inc(x1b2_ready, 1)
                if not final:
                    xbo(b + 1, k + p, 1 - p, False)

            nc.gpsimd.memset(ones[:, :], 1.0).then_inc(const_set, 1)
            nc.gpsimd.memset(minus_half[:, :], -0.5).then_inc(const_set, 1)
            k_over_tiles(0, True)
            xbo(0, 0, 0, True)
            pool.wait_ge(const_set, 2)
            run_slots(pool, slot)
            rstd(NB - 1, ve2, rstd2, ve2_done, rstd2_done)


def kernel(**inputs):
    import concourse.bacc as bacc
    from concourse.bass_utils import run_bass_kernel_spmd

    a = {n: np.asarray(v) for n, v in inputs.items()}
    x = a["L0_attn_x"]
    nb, s, d = x.shape
    f = a["L0_ffn_b1"].shape[0]
    nj = s // P
    row = lambda v: v.reshape(1, -1)
    heads_of = np.arange(P)[:, None] // (d // 16) == np.arange(P // (d // 16))[None, :]
    arrays = {
        "x": x,
        "x_t": x.reshape(nb, P, nj, d).transpose(0, 3, 2, 1).reshape(nb, d, s),
        "wqk_t": np.concatenate([a["L0_attn_Wq"].T, a["L0_attn_Wk"].T], axis=1),
        "bqk": row(np.concatenate([a["L0_attn_bq"], a["L0_attn_bk"]])),
        "wv_t": a["L0_attn_Wv"].T,
        "bv": a["L0_attn_bv"].reshape(d // P, P).T,
        "wo_t": a["L0_attn_Wo"].T,
        "bo": row(a["L0_attn_bo"]),
        "w1_t": a["L0_ffn_W1"].T,
        "b1": a["L0_ffn_b1"].reshape(f // P, P).T,
        "w2_t": a["L0_ffn_W2"].T,
        "b2": row(a["L0_ffn_b2"]),
        "ident_c": np.eye(P, dtype=np.float32),
        "mask_c": np.tile(heads_of, (1, d // P)).astype(np.float32),
    }
    arrays = {n: np.ascontiguousarray(v) for n, v in arrays.items()}
    nc = bacc.Bacc("TRN2", target_bir_lowering=False, num_devices=1)
    aps = [nc.dram_tensor(n, v.shape, mybir.dt.from_np(v.dtype), kind="ExternalInput").ap() for n, v in arrays.items()]
    out = nc.dram_tensor("out", (nb, s, d), F32, kind="ExternalOutput").ap()
    attention_ffn_block(nc, *aps, out)
    r = run_bass_kernel_spmd(nc, [arrays], core_ids=[0])
    return r.results[0]["out"]
```

```python
from contextlib import ExitStack

import numpy as np

import concourse.bass as bass
from concourse import mybir

F32 = mybir.dt.float32
F32R = mybir.dt.float32r
ALU = mybir.AluOpType
ACT = mybir.ActivationFunctionType
AX_X = mybir.AxisListType.X

P = 128
LN_EPS = 1e-5
Q_EPS = 1e-5
DEN_EPS = 1e-6


def attention_ffn_block(nc, x, x_t, wqk_t, bqk, wv_t, bv, wo_t, bo, w1_t, b1, w2_t, b2, ident_c, mask_c, out):
    NB, S, D = x.shape
    F = w1_t.shape[1]
    HEADS = 16
    HD = D // HEADS
    NJ = S // P
    ND = D // P
    NF = F // P
    NR = 4
    KV_AT, M_AT = NF // 2, 3 * NF // 4
    assert NJ == 4 and ND == 2 and NB % 2 == 0 and NB >= 4

    with ExitStack() as ctx:
        def sb(name, shape, dt=F32):
            return ctx.enter_context(nc.sbuf_tensor(name, shape, dt))

        def sem(name):
            return ctx.enter_context(nc.semaphore(name))

        wqk = sb("wqk", [P, ND, 2 * D])
        wv = sb("wv", [P, ND, D])
        wo = sb("wo", [P, ND, D])
        w1 = sb("w1", [P, ND * F])
        w2 = sb("w2", [P, NF * D])
        w1q = sb("w1q", [P, ND * F], F32R)
        w2q = sb("w2q", [P, NF * D], F32R)
        below = sb("below", [P, ND * F])
        bqk_rows = sb("bqk_rows", [P, 2 * D])
        bo_rows = sb("bo_rows", [P, D])
        b2_rows = sb("b2_rows", [P, D])
        bv_col = sb("bv_col", [P, ND])
        b1_col = sb("b1_col", [P, NF])
        ident = sb("ident", [P, P])
        mask = sb("mask", [P, HEADS])
        ones = sb("ones", [P, P])
        minus_half = sb("minus_half", [P, NJ])
        wsum = sb("wsum", [P, 2])
        thr = sb("thr", [P, 2])
        neg_thr = sb("neg_thr", [P, 2])

        xs = [sb(f"xs{p}", [P, NJ, D]) for p in range(2)]
        xt = [sb(f"xt{p}", [P, ND, S]) for p in range(2)]
        x_bo = sb("x_bo", [P, NJ, D])
        qk_pre = sb("qk_pre", [P, 2, 2 * D])
        qk_max = sb("qk_max", [P, 2, 2 * HEADS])
        qk_exp = sb("qk_exp", [P, NJ, 2 * D])
        k_pair = sb("k_pair", [P, 2, D])
        k_tok = sb("k_tok", [P, D])
        gt = sb("gt", [P, ND, D])
        k_sum = sb("k_sum", [P, D])
        qk_sum = sb("qk_sum", [P, NJ, D])
        den = sb("den", [P, NJ, HEADS])
        den_eps = sb("den_eps", [P, NJ, HEADS])
        rden = sb("rden", [P, NJ, HEADS])
        kv_raw = sb("kv_raw", [P, D])
        kv_t = sb("kv_t", [P, D])
        m = sb("m", [P, ND, D])
        q_t = sb("q_t", [P, ND, S])
        r1 = sb("r1", [P, NJ, D])
        st1 = sb("st1", [P, NJ, 6])
        mv1 = sb("mv1", [P, NJ, 2])
        ve1 = sb("ve1", [P, NJ])
        rstd1 = sb("rstd1", [P, NJ])
        shift1 = sb("shift1", [P, NJ])
        x1 = sb("x1", [P, NJ, D])
        x1_b2 = sb("x1_b2", [P, NJ, D])
        x1_hi = sb("x1_hi", [P, ND, S], F32R)
        x1_lo = sb("x1_lo", [P, ND, S], F32R)
        h_full = sb("h_full", [P, NR, S])
        h_hi = sb("h_hi", [P, NF, S], F32R)
        h_lo = sb("h_lo", [P, NF, S], F32R)
        r2 = sb("r2", [P, NJ, D])
        st2 = sb("st2", [P, NJ, 6])
        mv2 = sb("mv2", [P, NJ, 2])
        ve2 = sb("ve2", [P, NJ])
        rstd2 = sb("rstd2", [P, NJ])
        shift2 = sb("shift2", [P, NJ])
        res = [sb(f"res{p}", [P, NJ, D]) for p in range(2)]

        ps = ctx.enter_context(nc.psum_tensor("ps", [P, 8, 512], F32))
        WORK = 0
        MID = 2
        TOK = 4
        TRN = 6
        F1_BANKS = (WORK, WORK + 1, TRN, TRN + 1)
        s_w = {n: sem(f"s_{n}") for n in ("wqk", "bqk", "wv", "ident", "mask", "bv", "bo", "wo", "w1", "w2", "b1", "b2")}
        s_x = [sem(f"s_x{p}") for p in range(2)]
        s_xt = [sem(f"s_xt{p}") for p in range(2)]
        s_out = [sem(f"s_out{p}") for p in range(2)]
        const_set = sem("const_set")
        w_abs = sem("w_abs")
        w_total = sem("w_total")
        w_thr = sem("w_thr")
        w_below = sem("w_below")
        w_quant = sem("w_quant")
        qk_done = sem("qk_done")
        qk_added = sem("qk_added")
        qk_maxed = sem("qk_maxed")
        qk_shift = sem("qk_shift")
        exp_done = sem("exp_done")
        g_done = sem("g_done")
        gt_ready = sem("gt_ready")
        qt_done = sem("qt_done")
        qt_ready = sem("qt_ready")
        k_paired = sem("k_paired")
        k_tok_ready = sem("k_tok_ready")
        ksum_done = sem("ksum_done")
        ksum_ready = sem("ksum_ready")
        q_times_ksum = sem("q_times_ksum")
        den_ready = sem("den_ready")
        q_ready = sem("q_ready")
        kv_done = sem("kv_done")
        kv_biased = sem("kv_biased")
        kv_ready = sem("kv_ready")
        m_done = sem("m_done")
        m_ready = sem("m_ready")
        o_done = sem("o_done")
        xbo_ready = sem("xbo_ready")
        r1_done = sem("r1_done")
        st1_done = sem("st1_done")
        mv1_done = sem("mv1_done")
        ve1_done = sem("ve1_done")
        rstd1_done = sem("rstd1_done")
        shift1_done = sem("shift1_done")
        x1_ready = sem("x1_ready")
        x1b2_ready = sem("x1b2_ready")
        x1t_done = sem("x1t_done")
        x1hi_ready = sem("x1hi_ready")
        x1lo_ready = sem("x1lo_ready")
        f1_done = sem("f1_done")
        h_ready = sem("h_ready")
        hhi_odd = sem("hhi_odd")
        hlo_ready = sem("hlo_ready")
        f2_done = sem("f2_done")
        r2_done = sem("r2_done")
        st2_done = sem("st2_done")
        mv2_done = sem("mv2_done")
        ve2_done = sem("ve2_done")
        rstd2_done = sem("rstd2_done")
        shift2_done = sem("shift2_done")
        res_ready = sem("res_ready")

        def run_slots(eng, slot, peeled=1, last_looped=NB - 2):
            for b in range(peeled):
                slot(b // 2, b % 2)
            with eng.Fori(peeled // 2, last_looped // 2) as k:
                slot(k, 1)
                slot(k + 1, 0)
            for b in range(last_looped + 1, NB):
                slot(b // 2, b % 2)

        block = ctx.enter_context(nc.Block())

        @block.sync
        def _(sp):
            def load_xt(b, p):
                sp.dma_start(xt[p][:, :, :], x_t[b].rearrange("(c p) t -> p c t", p=P)).then_inc(s_xt[p], 16)

            def load_x(b, p):
                sp.dma_start(xs[p][:, :, :], x[b].rearrange("(p j) c -> p j c", j=NJ)).then_inc(s_x[p], 16)

            def weight(name, dst, src):
                sp.dma_start(dst, src).then_inc(s_w[name], 16)

            weight("wqk", wqk[:, :, :], wqk_t.rearrange("(c p) n -> p c n", p=P))
            load_xt(0, 0)
            weight("bqk", bqk_rows[:, :], bqk.to_broadcast([P, 2 * D]))
            load_xt(1, 1)
            load_x(0, 0)
            weight("wv", wv[:, :, :], wv_t.rearrange("(c p) n -> p c n", p=P))
            weight("bv", bv_col[:, :], bv)
            weight("mask", mask[:, :], mask_c)
            weight("w1", w1[:, :].rearrange("p (c n) -> p c n", c=ND), w1_t.rearrange("(c p) n -> p c n", p=P))
            weight("w2", w2[:, :].rearrange("p (c n) -> p c n", c=NF), w2_t.rearrange("(c p) n -> p c n", p=P))
            weight("bo", bo_rows[:, :], bo.to_broadcast([P, D]))
            weight("wo", wo[:, :, :], wo_t.rearrange("(c p) n -> p c n", p=P))
            weight("ident", ident[:, :], ident_c)
            load_x(1, 1)
            weight("b1", b1_col[:, :], b1)
            weight("b2", b2_rows[:, :], b2.to_broadcast([P, D]))

            def store(m, k, p):
                sp.wait_ge(res_ready, NJ * m + NJ)
                sp.dma_start(out[m].rearrange("(p j) c -> p j c", j=NJ), res[p][:, :, :]).then_inc(s_out[p], 16)

            def slot(k, p):
                b = 2 * k + p
                looped = not isinstance(b, int)
                if looped or b + 2 < NB:
                    sp.wait_ge(g_done, b + 1)
                    sp.wait_ge(xbo_ready, b + 1)
                    sp.wait_ge(qk_done, NJ * b + NJ)
                    load_xt(b + 2, p)
                    load_x(b + 2, p)
                if looped or b > 0:
                    store(b - 1, k - 1 + p, 1 - p)

            run_slots(sp, slot, last_looped=NB - 4)
            store(NB - 1, NB // 2 - 1, 1)
            for p in range(2):
                sp.wait_ge(s_out[p], 16 * (NB // 2))

        @block.tensor
        def _(pe):
            def mm(dst, lhs, rhs, start, stop):
                return nc.tensor.matmul(dst, lhs, rhs, start=start, stop=stop)

            def qk_tile(n, kn, pn, j):
                bank = ps[:, WORK + j % 2, :]
                if j >= 2:
                    pe.wait_ge(qk_added, NJ * n + j - 1)
                for c in range(ND):
                    last = mm(bank, xt[pn][:, c, j * P:(j + 1) * P], wqk[:, c, :], c == 0, c == ND - 1)
                last.then_inc(qk_done, 1)

            def k_total(n, first):
                pe.wait_ge(k_tok_ready, n + 1)
                if first:
                    pe.wait_ge(const_set, 2)
                mm(ps[:, MID + 1, 0:D], ones[:, :], k_tok[:, :], True, True).then_inc(ksum_done, 1)

            def g_and_k_total(n, kn, pn, first):
                if not first:
                    pe.wait_ge(r1_done, 2 * n)
                pe.wait_ge(exp_done, NJ * n + NJ)
                pe.wait_ge(s_x[pn], 16 * (kn + 1))
                for c in range(ND):
                    for j in range(NJ):
                        last = mm(ps[:, MID, c * D:(c + 1) * D], xs[pn][:, j, c * P:(c + 1) * P],
                                  qk_exp[:, j, D:2 * D], j == 0, j == NJ - 1)
                    if c == 0:
                        k_total(n, first)
                last.then_inc(g_done, 1)

            def kv_product(n):
                pe.wait_ge(ksum_ready, n + 1)
                pe.wait_ge(gt_ready, n + 1)
                for h in range(ND):
                    for c in range(ND):
                        last = mm(ps[:, MID + 1, h * P:(h + 1) * P], wv[:, c, h * P:(h + 1) * P],
                                  gt[:, c, h * P:(h + 1) * P], c == 0, c == ND - 1)
                last.then_inc(kv_done, 1)

            def m_product(n):
                pe.wait_ge(kv_ready, n + 1)
                for h in range(ND):
                    last = mm(ps[:, MID, h * D:(h + 1) * D], kv_t[:, h * P:(h + 1) * P], wo[:, h, :], True, True)
                last.then_inc(m_done, 1)

            def q_transpose(n, free):
                if not free:
                    pe.wait_ge(r2_done, 2 * n - 2)
                pe.wait_ge(q_ready, n + 1)
                for c in range(ND):
                    for j in range(NJ):
                        last = nc.tensor.transpose(ps[:, TOK + c, j * P:(j + 1) * P],
                                                   qk_exp[:, j, c * P:(c + 1) * P], ident[:, :])
                    last.then_inc(qt_done, 1)

            def ffn1(b, chunks):
                for f in chunks:
                    if f >= NR:
                        pe.wait_ge(h_ready, NF * b + f - NR + 1)
                    for c in range(ND):
                        for part in (x1_hi, x1_lo):
                            last = mm(ps[:, F1_BANKS[f % NR], :], w1q[:, c * F + f * P:c * F + (f + 1) * P],
                                      part[:, c, :], c == 0 and part is x1_hi, c == ND - 1 and part is x1_lo)
                    last.then_inc(f1_done, 1)

            def ffn2_part(dst, j, f, begin, end):
                for part in (h_hi, h_lo):
                    last = mm(dst, part[:, f, j * P:(j + 1) * P], w2q[:, f * D:(f + 1) * D],
                              begin and part is h_hi, end and part is h_lo)
                return last

            def ffn2(m, tiles):
                pe.wait_ge(hlo_ready, NF * m + NF)
                for j in tiles:
                    for f in range(NF):
                        last = ffn2_part(ps[:, TOK + j // 2, (j % 2) * D:(j % 2 + 1) * D], j, f, f == 0, f == NF - 1)
                    if j % 2 == 1:
                        last.then_inc(f2_done, 1)

            def ffn2_last(m):
                pe.wait_ge(r1_done, 2 * m + 2)
                pe.wait_ge(r2_done, 2 * m)
                for f in range(NF - 2):
                    pe.wait_ge(hlo_ready, NF * m + f + 1)
                    for j in range(NJ):
                        ffn2_part(ps[:, MID + j, 0:D], j, f, f == 0, False)
                pe.wait_ge(hlo_ready, NF * m + NF)
                for j in range(NJ):
                    for f in (NF - 2, NF - 1):
                        last = ffn2_part(ps[:, MID + j, 0:D], j, f, False, f == NF - 1)
                    if j % 2 == 1:
                        last.then_inc(f2_done, 1)

            def slot(k, p):
                b = 2 * k + p
                is_int = isinstance(b, int)
                first, final = is_int and b == 0, is_int and b == NB - 1
                n, kn, pn = b + 1, k + p, 1 - p
                if not final and not first:
                    pe.wait_ge(s_xt[pn], 16 * (kn + 1))
                    pe.wait_ge(h_ready, NF * b - 3)
                    qk_tile(n, kn, pn, 0)
                    pe.wait_ge(h_ready, NF * b - 2)
                    qk_tile(n, kn, pn, 1)
                if first:
                    pe.wait_ge(s_w["wo"], 16)
                    m_product(0)
                    pe.wait_ge(s_w["ident"], 16)
                    q_transpose(0, True)
                    pe.wait_ge(w_abs, 2)
                    mm(ps[:, TRN, 0:2], ones[:, :], wsum[:, :], True, True).then_inc(w_total, 1)
                pe.wait_ge(m_ready, b + 1)
                pe.wait_ge(kv_biased, ND * b + ND)
                pe.wait_ge(qt_ready, ND * b + ND)
                for j in range(NJ):
                    for c in range(ND):
                        last = mm(ps[:, MID + j // 2, (j % 2) * D:(j % 2 + 1) * D],
                                  q_t[:, c, j * P:(j + 1) * P], m[:, c, :], c == 0, c == ND - 1)
                    if j % 2 == 1:
                        last.then_inc(o_done, 1)
                if not final:
                    qk_tile(n, kn, pn, 2)
                    qk_tile(n, kn, pn, 3)
                if final:
                    ffn2(b - 1, range(NJ - 1))
                elif not first:
                    ffn2(b - 1, range(NJ))
                pe.wait_ge(x1_ready, NJ * b + NJ)
                if first:
                    pe.wait_ge(w_thr, 1)
                else:
                    pe.wait_ge(h_ready, NF * b)
                for c in range(ND):
                    for j in range(NJ):
                        last = nc.tensor.transpose(ps[:, TRN + c, j * P:(j + 1) * P],
                                                   x1[:, j, c * P:(c + 1) * P], ident[:, :])
                    last.then_inc(x1t_done, 1)
                if final:
                    ffn2(b - 1, range(NJ - 1, NJ))
                if not final:
                    g_and_k_total(n, kn, pn, False)
                if first:
                    pe.wait_ge(w_quant, 1)
                pe.wait_ge(x1lo_ready, ND * b + ND)
                if not final:
                    pe.wait_ge(qk_added, NJ * n + NJ)
                ffn1(b, range(KV_AT))
                if not final:
                    kv_product(n)
                ffn1(b, range(KV_AT, M_AT))
                if not final:
                    m_product(n)
                    q_transpose(n, first)
                ffn1(b, range(M_AT, NF))

            pe.wait_ge(s_w["wqk"], 16)
            pe.wait_ge(s_xt[0], 16)
            for j in range(NJ):
                qk_tile(0, 0, 0, j)
            pe.wait_ge(s_xt[1], 16)
            pe.wait_ge(qk_added, NJ - 1)
            qk_tile(1, 0, 1, 0)
            pe.wait_ge(qk_added, NJ)
            qk_tile(1, 0, 1, 1)
            g_and_k_total(0, 0, 0, True)
            pe.wait_ge(s_w["wv"], 16)
            kv_product(0)
            run_slots(pe, slot)
            ffn2_last(NB - 1)

        @block.scalar
        def _(act):
            def exp_tile(n, j):
                act.wait_ge(qk_shift, NJ * n + j + 1)
                nc.scalar.activation(qk_exp[:, j, :], qk_pre[:, j % 2, :], ACT.Exp).then_inc(exp_done, 1)

            def m_and_qt(n, first):
                act.wait_ge(m_done, n + 1)
                if not first:
                    act.wait_ge(o_done, 2 * n)
                nc.scalar.copy(m[:, :, :], ps[:, MID, :].rearrange("p (c d) -> p c d", c=ND)).then_inc(m_ready, 1)
                for c in range(ND):
                    act.wait_ge(qt_done, ND * n + c + 1)
                    nc.scalar.copy(q_t[:, c, :], ps[:, TOK + c, :]).then_inc(qt_ready, 1)

            def k_sum_out(n, first):
                act.wait_ge(ksum_done, n + 1)
                if not first:
                    act.wait_ge(kv_biased, ND * n)
                nc.scalar.copy(k_sum[:, :], ps[:, MID + 1, 0:D]).then_inc(ksum_ready, 1)

            def gt_out(n, first):
                act.wait_ge(g_done, n + 1)
                if not first:
                    act.wait_ge(kv_done, n)
                nc.scalar.copy(gt[:, :, :], ps[:, MID, :].rearrange("p (c d) -> p c d", c=ND)).then_inc(gt_ready, 1)

            def normalise(dst, r, rstd, shift, ready):
                for j in range(NJ):
                    nc.scalar.activation(dst[:, j, :], r[:, j, :], ACT.Identity, scale=rstd[:, j:j + 1],
                                         bias=shift[:, j:j + 1]).then_inc(ready, 1)

            def normalise2(mb, km, pm, early):
                act.wait_ge(shift2_done, mb + 1)
                if not early:
                    act.wait_ge(s_out[pm], 16 * km)
                normalise(res[pm], r2, rstd2, shift2, res_ready)

            def hidden(b, first, chunks):
                for f in chunks:
                    act.wait_ge(f1_done, NF * b + f + 1)
                    if not first or f >= NR:
                        act.wait_ge(hlo_ready, NF * b + f - NR + 1)
                    bank, bias = ps[:, F1_BANKS[f % NR], :], b1_col[:, f:f + 1]
                    if f % 2 == 0:
                        nc.scalar.activation(h_hi[:, f, :], bank, ACT.Relu, bias=bias)
                    nc.scalar.activation(h_full[:, f % NR, :], bank, ACT.Relu, bias=bias).then_inc(h_ready, 1)

            def slot(k, p):
                b = 2 * k + p
                is_int = isinstance(b, int)
                first, final = is_int and b == 0, is_int and b == NB - 1
                n = b + 1
                if first:
                    m_and_qt(0, True)
                if not final:
                    act.wait_ge(g_done, n)
                    act.wait_ge(qt_done, ND * n)
                    act.wait_ge(k_paired, n)
                    for j in range(3):
                        exp_tile(n, j)
                act.wait_ge(shift1_done, b + 1)
                if not first:
                    act.wait_ge(x1t_done, ND * b)
                    act.wait_ge(x1b2_ready, b)
                normalise(x1, r1, rstd1, shift1, x1_ready)
                if not final:
                    exp_tile(n, 3)
                if not first:
                    act.wait_ge(f1_done, NF * b)
                for c in range(ND):
                    act.wait_ge(x1t_done, ND * b + c + 1)
                    nc.scalar.copy(x1_hi[:, c, :], ps[:, TRN + c, :]).then_inc(x1hi_ready, 1)
                if not final:
                    k_sum_out(n, False)
                    gt_out(n, False)
                if first:
                    act.wait_ge(s_w["b1"], 16)
                else:
                    act.wait_ge(f2_done, 2 * b)
                hidden(b, first, range(2))
                if not first and not final:
                    normalise2(b - 1, k - 1 + p, 1 - p, is_int and b <= 2)
                hidden(b, first, range(2, M_AT))
                if not final:
                    m_and_qt(n, False)
                hidden(b, first, range(M_AT, NF))
                if final:
                    normalise2(b - 1, k - 1 + p, 1 - p, False)

            for j in range(NJ):
                exp_tile(0, j)
            k_sum_out(0, True)
            gt_out(0, True)
            for i, (name, w, scratch) in enumerate((("w1", w1, w1q), ("w2", w2, w2q))):
                act.wait_ge(s_w[name], 16)
                nc.scalar.activation(scratch[:, :], w[:, :], ACT.Abs, accum_out=wsum[:, i:i + 1]).then_inc(w_abs, 1)
            run_slots(act, slot, peeled=3)
            normalise2(NB - 1, NB // 2 - 1, 1, False)

        @block.vector
        def _(dve):
            def qk_add(n, j, first=False):
                dve.wait_ge(qk_done, NJ * n + j + 1)
                if not first or j >= 2:
                    dve.wait_ge(exp_done, NJ * n + j - 1)
                nc.vector.tensor_tensor(qk_pre[:, j % 2, :], ps[:, WORK + j % 2, :], bqk_rows[:, :],
                                        ALU.add).then_inc(qk_added, 1)

            def qk_top(n, j):
                heads = qk_pre[:, j % 2, :].rearrange("p (h e) -> p h e", e=HD)
                dve.wait_ge(qk_added, NJ * n + j + 1)
                nc.vector.tensor_reduce(qk_max[:, j % 2, :], heads, AX_X, ALU.max).then_inc(qk_maxed, 1)

            def qk_less_top(n, j):
                heads = qk_pre[:, j % 2, :].rearrange("p (h e) -> p h e", e=HD)
                dve.wait_ge(qk_maxed, NJ * n + j + 1)
                nc.vector.tensor_tensor(heads, heads, qk_max[:, j % 2, :].unsqueeze(2).to_broadcast([P, 2 * HEADS, HD]),
                                        ALU.subtract).then_inc(qk_shift, 1)

            def q_normalise(n):
                q = qk_exp[:, :, 0:D]
                dve.wait_ge(exp_done, NJ * n + NJ)
                dve.wait_ge(ksum_ready, n + 1)
                nc.vector.tensor_tensor(qk_sum[:, :, :], q, k_sum[:, :].unsqueeze(1).to_broadcast([P, NJ, D]),
                                        ALU.mult).then_inc(q_times_ksum, 1)
                dve.wait_ge(q_times_ksum, n + 1)
                nc.vector.tensor_reduce(den[:, :, :].rearrange("p j h -> p (j h)"),
                                        qk_sum[:, :, :].rearrange("p j (h e) -> p (j h) e", e=HD), AX_X,
                                        ALU.add).then_inc(den_ready, 1)
                dve.wait_ge(den_ready, 3 * n + 1)
                nc.vector.tensor_scalar(den_eps[:, :, :], den[:, :, :], DEN_EPS, None, ALU.add).then_inc(den_ready, 1)
                dve.wait_ge(den_ready, 3 * n + 2)
                nc.vector.reciprocal(rden[:, :, :], den_eps[:, :, :]).then_inc(den_ready, 1)
                dve.wait_ge(den_ready, 3 * n + 3)
                for j in range(NJ):
                    q_heads = q[:, j, :].rearrange("p (h e) -> p h e", e=HD)
                    last = nc.vector.tensor_tensor(q_heads, q_heads,
                                                   rden[:, j, :].unsqueeze(2).to_broadcast([P, HEADS, HD]), ALU.mult)
                last.then_inc(q_ready, 1)

            def kv_finish(n, first):
                dve.wait_ge(kv_done, n + 1)
                for h in range(ND):
                    d = slice(h * P, (h + 1) * P)
                    nc.vector.scalar_tensor_tensor(kv_raw[:, d], k_sum[:, d], bv_col[:, h:h + 1], ps[:, MID + 1, d],
                                                   ALU.mult, ALU.add).then_inc(kv_biased, 1)
                if not first:
                    dve.wait_ge(m_done, n)
                dve.wait_ge(kv_biased, ND * n + ND)
                nc.vector.tensor_tensor(kv_t[:, :].rearrange("p (h e) -> p h e", e=HD),
                                        kv_raw[:, :].rearrange("p (h e) -> p h e", e=HD),
                                        mask[:, :].unsqueeze(2).to_broadcast([P, HEADS, HD]),
                                        ALU.mult).then_inc(kv_ready, 1)

            def row_stats(r, st, st_done):
                for j in range(NJ):
                    nc.vector.bn_stats(st[:, j, :], r[:, j, :]).then_inc(st_done, 1)

            def row_moments(st, mv, ve, mv_done, ve_done, b):
                for j in range(NJ):
                    nc.vector.bn_aggr(mv[:, j, :], st[:, j, :]).then_inc(mv_done, 1)
                dve.wait_ge(mv_done, NJ * b + NJ)
                nc.vector.tensor_scalar(ve[:, :], mv[:, :, 1], LN_EPS, None, ALU.add).then_inc(ve_done, 1)

            def h_low(b, chunks):
                for f in chunks:
                    dve.wait_ge(h_ready, NF * b + f + 1)
                    if f % 2 == 1:
                        nc.vector.tensor_copy(h_hi[:, f, :], h_full[:, f % NR, :]).then_inc(hhi_odd, 1)
                        dve.wait_ge(hhi_odd, NF // 2 * b + f // 2 + 1)
                    nc.vector.tensor_tensor(h_lo[:, f, :], h_full[:, f % NR, :], h_hi[:, f, :].bitcast(F32),
                                            ALU.subtract).then_inc(hlo_ready, 1)

            def residual2(m):
                dve.wait_ge(x1b2_ready, m + 1)
                if not isinstance(m, int) or m > 0:
                    dve.wait_ge(res_ready, NJ * m)
                last = isinstance(m, int) and m == NB - 1
                for t in range(2):
                    tiles = slice(2 * t, 2 * t + 2)
                    f2 = ps[:, TOK + t, :].rearrange("p (j c) -> p j c", j=2)
                    if last:
                        f2 = ps[:, MID + 2 * t:MID + 2 * t + 2, 0:D]
                    dve.wait_ge(f2_done, 2 * m + t + 1)
                    nc.vector.tensor_tensor(r2[:, tiles, :], f2, x1_b2[:, tiles, :], ALU.add).then_inc(r2_done, 1)
                dve.wait_ge(r2_done, 2 * m + 2)
                row_stats(r2, st2, st2_done)

            def x1_low(b):
                if not isinstance(b, int) or b > 0:
                    dve.wait_ge(f1_done, NF * b)
                for c in range(ND):
                    dve.wait_ge(x1hi_ready, ND * b + c + 1)
                    nc.vector.tensor_tensor(x1_lo[:, c, :], ps[:, TRN + c, :], x1_hi[:, c, :].bitcast(F32),
                                            ALU.subtract).then_inc(x1lo_ready, 1)

            def shift(mv, rstd, sh, rstd_done, sh_done, b):
                dve.wait_ge(rstd_done, b + 1)
                nc.vector.scalar_tensor_tensor(sh[:, :], mv[:, :, 0], -1.0, rstd[:, :], ALU.mult,
                                               ALU.mult).then_inc(sh_done, 1)

            def slot(k, p):
                b = 2 * k + p
                is_int = isinstance(b, int)
                first, final = is_int and b == 0, is_int and b == NB - 1
                n = b + 1
                if not final:
                    qk_add(n, 0)
                    qk_add(n, 1)
                    qk_top(n, 0)
                    qk_top(n, 1)
                    qk_less_top(n, 0)
                    qk_less_top(n, 1)
                if first:
                    thresholds()
                    quantise(0, w1, w1q)
                dve.wait_ge(xbo_ready, b + 1)
                if not first:
                    dve.wait_ge(x1_ready, NJ * b)
                for t in range(2):
                    dve.wait_ge(o_done, 2 * b + t + 1)
                    nc.vector.tensor_tensor(r1[:, 2 * t:2 * t + 2, :].rearrange("p j c -> p (j c)"), ps[:, MID + t, :],
                                            x_bo[:, 2 * t:2 * t + 2, :].rearrange("p j c -> p (j c)"),
                                            ALU.add).then_inc(r1_done, 1)
                dve.wait_ge(r1_done, 2 * b + 2)
                row_stats(r1, st1, st1_done)
                dve.wait_ge(st1_done, NJ * b + NJ)
                if not final:
                    qk_add(n, 2)
                row_moments(st1, mv1, ve1, mv1_done, ve1_done, b)
                if not final:
                    qk_top(n, 2)
                    qk_add(n, 3)
                    qk_less_top(n, 2)
                    shift(mv1, rstd1, shift1, rstd1_done, shift1_done, b)
                    qk_top(n, 3)
                    qk_less_top(n, 3)
                else:
                    shift(mv1, rstd1, shift1, rstd1_done, shift1_done, b)
                if final:
                    x1_low(b)
                    dve.wait_ge(f2_done, 2 * b)
                    h_low(b, range(2))
                    residual2(b - 1)
                    dve.wait_ge(st2_done, NJ * b)
                elif first:
                    x1_low(b)
                    quantise(1, w2, w2q)
                else:
                    residual2(b - 1)
                    dve.wait_ge(st2_done, NJ * b)
                    x1_low(b)
                if not first:
                    row_moments(st2, mv2, ve2, mv2_done, ve2_done, b - 1)
                if not final:
                    q_normalise(n)
                if final:
                    h_low(b, range(2, NF))
                if not first:
                    shift(mv2, rstd2, shift2, rstd2_done, shift2_done, b - 1)
                    dve.wait_ge(f2_done, 2 * b)
                if not final:
                    kv_finish(n, False)
                    h_low(b, range(NF))

            def thresholds():
                dve.wait_ge(w_total, 1)
                nc.vector.tensor_scalar(thr[:, :], ps[:, TRN, 0:2], 1.0 / (D * F), Q_EPS,
                                        ALU.mult, ALU.add).then_inc(w_thr, 1)
                dve.wait_ge(w_thr, 1)
                nc.vector.tensor_scalar(neg_thr[:, :], thr[:, :], -0.5, None, ALU.mult).then_inc(w_thr, 1)
                dve.wait_ge(w_thr, 2)
                nc.vector.tensor_scalar(thr[:, :], thr[:, :], 0.5, None, ALU.mult).then_inc(w_thr, 1)

            def quantise(i, w, wq):
                if i == 0:
                    dve.wait_ge(w_thr, 3)
                else:
                    dve.wait_ge(w_quant, i)
                nc.vector.tensor_scalar(below[:, :], w[:, :], neg_thr[:, i:i + 1], None,
                                        ALU.is_lt).then_inc(w_below, 1)
                dve.wait_ge(w_below, i + 1)
                nc.vector.scalar_tensor_tensor(wq[:, :], w[:, :], thr[:, i:i + 1], below[:, :],
                                               ALU.is_gt, ALU.subtract).then_inc(w_quant, 1)

            dve.wait_ge(s_w["bqk"], 16)
            for j in range(NJ):
                qk_add(0, j, first=True)
                qk_top(0, j)
                qk_less_top(0, j)
            q_normalise(0)
            dve.wait_ge(s_w["bv"], 16)
            dve.wait_ge(s_w["mask"], 16)
            kv_finish(0, True)
            run_slots(dve, slot, peeled=3)
            residual2(NB - 1)
            dve.wait_ge(st2_done, NJ * NB)
            row_moments(st2, mv2, ve2, mv2_done, ve2_done, NB - 1)
            shift(mv2, rstd2, shift2, rstd2_done, shift2_done, NB - 1)

        @block.gpsimd
        def _(pool):
            def xbo(n, kn, pn, first):
                pool.wait_ge(s_x[pn], 16 * (kn + 1))
                if first:
                    pool.wait_ge(s_w["bo"], 16)
                else:
                    pool.wait_ge(r1_done, 2 * n)
                nc.gpsimd.tensor_tensor(x_bo[:, :, :], xs[pn][:, :, :], bo_rows[:, :].unsqueeze(1).to_broadcast([P, NJ, D]),
                                        ALU.add).then_inc(xbo_ready, 1)

            def k_over_tiles(n, first):
                pool.wait_ge(exp_done, NJ * n + NJ)
                nc.gpsimd.tensor_tensor(k_pair[:, :, :], qk_exp[:, 0:2, D:2 * D], qk_exp[:, 2:4, D:2 * D],
                                        ALU.add).then_inc(k_paired, 1)
                pool.wait_ge(k_paired, n + 1)
                if not first:
                    pool.wait_ge(ksum_done, n)
                nc.gpsimd.tensor_tensor(k_tok[:, :], k_pair[:, 0, :], k_pair[:, 1, :], ALU.add).then_inc(k_tok_ready, 1)

            def rstd(b, ve, r, ve_done, r_done):
                pool.wait_ge(ve_done, b + 1)
                nc.gpsimd.tensor_tensor(r[:, :], ve[:, :], minus_half[:, :], ALU.pow).then_inc(r_done, 1)

            def slot(k, p):
                b = 2 * k + p
                is_int = isinstance(b, int)
                first, final = is_int and b == 0, is_int and b == NB - 1
                rstd(b, ve1, rstd1, ve1_done, rstd1_done)
                if not final:
                    k_over_tiles(b + 1, False)
                if not first:
                    rstd(b - 1, ve2, rstd2, ve2_done, rstd2_done)
                pool.wait_ge(x1_ready, NJ * b + NJ)
                if first:
                    pool.wait_ge(s_w["b2"], 16)
                else:
                    pool.wait_ge(r2_done, 2 * b)
                nc.gpsimd.tensor_tensor(x1_b2[:, :, :], x1[:, :, :], b2_rows[:, :].unsqueeze(1).to_broadcast([P, NJ, D]),
                                        ALU.add).then_inc(x1b2_ready, 1)
                if not final:
                    xbo(b + 1, k + p, 1 - p, False)

            nc.gpsimd.memset(ones[:, :], 1.0).then_inc(const_set, 1)
            nc.gpsimd.memset(minus_half[:, :], -0.5).then_inc(const_set, 1)
            k_over_tiles(0, True)
            xbo(0, 0, 0, True)
            pool.wait_ge(const_set, 2)
            run_slots(pool, slot)
            rstd(NB - 1, ve2, rstd2, ve2_done, rstd2_done)


def kernel(**inputs):
    import concourse.bacc as bacc
    from concourse.bass_utils import run_bass_kernel_spmd

    a = {n: np.asarray(v) for n, v in inputs.items()}
    x = a["L0_attn_x"]
    nb, s, d = x.shape
    f = a["L0_ffn_b1"].shape[0]
    nj = s // P
    row = lambda v: v.reshape(1, -1)
    heads_of = np.arange(P)[:, None] // (d // 16) == np.arange(P // (d // 16))[None, :]
    arrays = {
        "x": x,
        "x_t": x.reshape(nb, P, nj, d).transpose(0, 3, 2, 1).reshape(nb, d, s),
        "wqk_t": np.concatenate([a["L0_attn_Wq"].T, a["L0_attn_Wk"].T], axis=1),
        "bqk": row(np.concatenate([a["L0_attn_bq"], a["L0_attn_bk"]])),
        "wv_t": a["L0_attn_Wv"].T,
        "bv": a["L0_attn_bv"].reshape(d // P, P).T,
        "wo_t": a["L0_attn_Wo"].T,
        "bo": row(a["L0_attn_bo"]),
        "w1_t": a["L0_ffn_W1"].T,
        "b1": a["L0_ffn_b1"].reshape(f // P, P).T,
        "w2_t": a["L0_ffn_W2"].T,
        "b2": row(a["L0_ffn_b2"]),
        "ident_c": np.eye(P, dtype=np.float32),
        "mask_c": np.tile(heads_of, (1, d // P)).astype(np.float32),
    }
    arrays = {n: np.ascontiguousarray(v) for n, v in arrays.items()}
    nc = bacc.Bacc("TRN2", target_bir_lowering=False, num_devices=1)
    aps = [nc.dram_tensor(n, v.shape, mybir.dt.from_np(v.dtype), kind="ExternalInput").ap() for n, v in arrays.items()]
    out = nc.dram_tensor("out", (nb, s, d), F32, kind="ExternalOutput").ap()
    attention_ffn_block(nc, *aps, out)
    r = run_bass_kernel_spmd(nc, [arrays], core_ids=[0])
    return r.results[0]["out"]
```
